# Optimizing a Trainium2 kernel written in Bass

```python
import numpy as np
import jax
import jax.numpy as jnp

def _softmax(x, axis=-1):
    return jax.nn.softmax(x, axis=axis)

def _gelu(x):
    return jax.nn.gelu(x, approximate=True)

def _silu(x):
    return jax.nn.silu(x)

def _sigmoid(x):
    return jax.nn.sigmoid(x)

def _layernorm(x, axis=-1, eps=1e-05):
    m = jnp.mean(x, axis=axis, keepdims=True)
    v = jnp.var(x, axis=axis, keepdims=True)
    return (x - m) / jnp.sqrt(v + eps)

def _scatter_add(tgt, idx, src, axis=0):
    return tgt.at[idx].add(src)

def _segment_sum(src, seg, n):
    return jax.ops.segment_sum(src, seg, n)
kernel_name = 'mk_xattn_ffn_d1_seqx_r8_28f6a3'

def setup_inputs(seed: int=0):
    np.random.seed(seed)
    _w = jnp.asarray

    def _rec_inputs():
        import jax
        import jax.numpy as jnp
        _rk = jax.random.key(seed)
        x = -0.0005146 + 1 * jax.random.normal(jax.random.fold_in(_rk, 1), (8, 256, 128), jnp.float32)
        _lenS = 256 - jax.random.randint(jax.random.fold_in(_rk, 7), (8,), 0, max(1, 256 // 4) + 1, jnp.int32)
        _lenS2 = 512 - jax.random.randint(jax.random.fold_in(_rk, 8), (8,), 0, max(1, 512 // 4) + 1, jnp.int32)
        _ctx_768P = jax.random.normal(jax.random.fold_in(_rk, 11), (8, 16, 96), jnp.float32)
        _ctx_768c = jax.random.dirichlet(jax.random.fold_in(_rk, 511), 0.3 * jnp.ones((16,), jnp.float32), (8, 512))
        _ctx_768t = jnp.einsum('bsk,bkd->bsd', _ctx_768c, _ctx_768P)
        _ctx_768t = _ctx_768t * jax.lax.rsqrt(jnp.mean(jnp.square(_ctx_768t)) + 1e-12) * 0.953939
        ctx_768 = -0.00040386 + 0.999972 * (_ctx_768t + 0.3 * jax.random.normal(jax.random.fold_in(_rk, 611), (8, 512, 96), jnp.float32))
        _validS = jnp.arange(256)[None, :] < _lenS[:, None]
        _validS2 = jnp.arange(512)[None, :] < _lenS2[:, None]
        _causal = jnp.tril(jnp.ones((256, 256), dtype=bool))
        mask_BxS2_bk0 = jnp.logical_not(jnp.broadcast_to(_validS2[:, :], (8, 512)))
        return (x, ctx_768, mask_BxS2_bk0)
    x, ctx_768, mask_BxS2_bk0 = _rec_inputs()

    def _L0_xattn_setup():
        import jax, jax.numpy as jnp
        import numpy as np
        DIM_IN, DIM_LAT, DIM_HEAD = (96, 128, 64)
        INNER = max(DIM_LAT, DIM_IN)
        HEADS = INNER // DIM_HEAD
        SCALE = DIM_HEAD ** (-0.5)
        RMS_EPS = 1e-08
        LN_EPS = 1e-05

        def layernorm(x, g, b):
            mu = jnp.mean(x, axis=-1, keepdims=True)
            var = jnp.mean((x - mu) ** 2, axis=-1, keepdims=True)
            return (x - mu) * jax.lax.rsqrt(var + LN_EPS) * g + b

        def rmsnorm(x, gamma):
            norm = jnp.sqrt(jnp.sum(x * x, axis=-1, keepdims=True)) * x.shape[-1] ** (-0.5)
            return x / jnp.maximum(norm, RMS_EPS) * gamma
        key = jax.random.key(seed)
        ks = jax.random.split(key, 12)
        b, n, m = (4, 512, 64)
        x = jax.random.normal(ks[0], (b, n, DIM_IN), jnp.float32)
        latents = jax.random.normal(ks[1], (b, m, DIM_LAT), jnp.float32)
        mask = jax.random.randint(ks[2], (b, n), 0, 2).astype(bool)
        s = lambda k, sh, fan: jax.random.normal(k, sh, jnp.float32) * fan ** (-0.5)
        return {'x': x, 'latents': latents, 'mask': mask, 'ln_x_g': jnp.ones((DIM_IN,), jnp.float32), 'ln_x_b': jnp.zeros((DIM_IN,), jnp.float32), 'ln_l_g': jnp.ones((DIM_LAT,), jnp.float32), 'ln_l_b': jnp.zeros((DIM_LAT,), jnp.float32), 'qn_g': jnp.ones((DIM_HEAD,), jnp.float32), 'kn_g': jnp.ones((DIM_HEAD,), jnp.float32), 'Wq': s(ks[3], (INNER, DIM_LAT), DIM_LAT), 'Wkv': s(ks[4], (2 * INNER, DIM_IN), DIM_IN), 'Wlkv': s(ks[5], (2 * INNER, DIM_LAT), DIM_LAT), 'Wo': s(ks[6], (DIM_LAT, INNER), INNER), 'bo': jnp.zeros((DIM_LAT,), jnp.float32)}
    _L0_xattn_all = _L0_xattn_setup()
    _L0_xattn_in = {k: v for k, v in _L0_xattn_all.items() if k in ('ln_x_g', 'ln_x_b', 'ln_l_g', 'ln_l_b', 'qn_g', 'kn_g', 'Wq', 'Wkv', 'Wlkv', 'Wo', 'bo')}
    del _L0_xattn_all

    def _L0_ffn_setup():
        import jax, jax.numpy as jnp
        import numpy as np
        E = 8
        K = 2
        D = 128
        H = 342
        B, S = (2, 256)

        def _moe_forward(x, centroid, Wg, bg, W1, b1, W2, b2):
            T = x.shape[0] * x.shape[1]
            xs = x.reshape(T, D)
            d2 = jnp.sum(xs * xs, axis=-1, keepdims=True) + jnp.sum(centroid * centroid, axis=-1)[None, :] - 2.0 * (xs @ centroid.T)
            dist = jnp.sqrt(jnp.maximum(d2, 1e-12))
            w, sel = jax.lax.top_k(dist, K)
            w = jax.nn.softmax(w.astype(jnp.float32), axis=1).astype(x.dtype)
            we = jnp.zeros((T, E), dtype=x.dtype).at[jnp.arange(T)[:, None], sel].add(w)
            out = jnp.zeros_like(xs)
            for e in range(E):
                h = jax.nn.silu(xs @ Wg[e] + bg[e]) * (xs @ W1[e] + b1[e])
                out = out + we[:, e:e + 1] * (h @ W2[e] + b2[e])
            return out.reshape(x.shape)
        key = jax.random.key(seed)
        ks = jax.random.split(key, 9)
        scale = 0.02
        return {'x': jax.random.normal(ks[0], (B, S, D), dtype=jnp.float32), 'centroid': jax.random.normal(ks[1], (E, D), dtype=jnp.float32), 'Wg': jax.random.normal(ks[2], (E, D, H), dtype=jnp.float32) * scale, 'bg': jnp.zeros((E, H), dtype=jnp.float32), 'W1': jax.random.normal(ks[3], (E, D, H), dtype=jnp.float32) * scale, 'b1': jnp.zeros((E, H), dtype=jnp.float32), 'W2': jax.random.normal(ks[4], (E, H, D), dtype=jnp.float32) * scale, 'b2': jnp.zeros((E, D), dtype=jnp.float32)}
    _L0_ffn_all = _L0_ffn_setup()
    _L0_ffn_in = {k: v for k, v in _L0_ffn_all.items() if k in ('centroid', 'Wg', 'bg', 'W1', 'b1', 'W2', 'b2')}
    del _L0_ffn_all
    return {'x': x, 'ctx_768': ctx_768, 'mask_BxS2_bk0': mask_BxS2_bk0, 'L0_xattn_ln_x_g': _L0_xattn_in['ln_x_g'], 'L0_xattn_ln_x_b': _L0_xattn_in['ln_x_b'], 'L0_xattn_ln_l_g': _L0_xattn_in['ln_l_g'], 'L0_xattn_ln_l_b': _L0_xattn_in['ln_l_b'], 'L0_xattn_qn_g': _L0_xattn_in['qn_g'], 'L0_xattn_kn_g': _L0_xattn_in['kn_g'], 'L0_xattn_Wq': _L0_xattn_in['Wq'], 'L0_xattn_Wkv': _L0_xattn_in['Wkv'], 'L0_xattn_Wlkv': _L0_xattn_in['Wlkv'], 'L0_xattn_Wo': _L0_xattn_in['Wo'], 'L0_xattn_bo': _L0_xattn_in['bo'], 'L0_ffn_centroid': _L0_ffn_in['centroid'], 'L0_ffn_Wg': _L0_ffn_in['Wg'], 'L0_ffn_bg': _L0_ffn_in['bg'], 'L0_ffn_W1': _L0_ffn_in['W1'], 'L0_ffn_b1': _L0_ffn_in['b1'], 'L0_ffn_W2': _L0_ffn_in['W2'], 'L0_ffn_b2': _L0_ffn_in['b2']}

def reference(x, ctx_768, mask_BxS2_bk0, L0_xattn_ln_x_g, L0_xattn_ln_x_b, L0_xattn_ln_l_g, L0_xattn_ln_l_b, L0_xattn_qn_g, L0_xattn_kn_g, L0_xattn_Wq, L0_xattn_Wkv, L0_xattn_Wlkv, L0_xattn_Wo, L0_xattn_bo, L0_ffn_centroid, L0_ffn_Wg, L0_ffn_bg, L0_ffn_W1, L0_ffn_b1, L0_ffn_W2, L0_ffn_b2):
    import jax
    import jax.numpy as jnp

    def _L0_xattn_ref(x, latents, mask, ln_x_g, ln_x_b, ln_l_g, ln_l_b, qn_g, kn_g, Wq, Wkv, Wlkv, Wo, bo):
        import jax, jax.numpy as jnp
        import numpy as np
        DIM_IN, DIM_LAT, DIM_HEAD = (96, 128, 64)
        INNER = max(DIM_LAT, DIM_IN)
        HEADS = INNER // DIM_HEAD
        SCALE = DIM_HEAD ** (-0.5)
        RMS_EPS = 1e-08
        LN_EPS = 1e-05

        def layernorm(x, g, b):
            mu = jnp.mean(x, axis=-1, keepdims=True)
            var = jnp.mean((x - mu) ** 2, axis=-1, keepdims=True)
            return (x - mu) * jax.lax.rsqrt(var + LN_EPS) * g + b

        def rmsnorm(x, gamma):
            norm = jnp.sqrt(jnp.sum(x * x, axis=-1, keepdims=True)) * x.shape[-1] ** (-0.5)
            return x / jnp.maximum(norm, RMS_EPS) * gamma
        b, n, _ = x.shape
        m = latents.shape[1]
        xn = layernorm(x, ln_x_g, ln_x_b)
        ln = layernorm(latents, ln_l_g, ln_l_b)
        q = ln @ Wq.T
        kv = jnp.concatenate([xn @ Wkv.T, ln @ Wlkv.T], axis=1)
        k, v = (kv[..., :INNER], kv[..., INNER:])
        split_heads = lambda t: t.reshape(t.shape[0], t.shape[1], HEADS, DIM_HEAD).transpose(0, 2, 1, 3)
        q, k, v = (split_heads(q), split_heads(k), split_heads(v))
        qn = rmsnorm(q, qn_g) * SCALE
        kn = rmsnorm(k, kn_g)
        attn = jnp.einsum('bhid,bhjd->bhij', qn, kn)
        full_mask = jnp.pad(mask, ((0, 0), (0, m)), constant_values=True)
        attn = jnp.where(full_mask[:, None, None, :], attn, -jnp.finfo(attn.dtype).max)
        attn = jax.nn.softmax(attn, axis=-1)
        out = jnp.einsum('bhij,bhjd->bhid', attn, v)
        out = out.transpose(0, 2, 1, 3).reshape(b, m, INNER)
        return out @ Wo.T + bo

    def _L0_ffn_ref(x, centroid, Wg, bg, W1, b1, W2, b2):
        import jax, jax.numpy as jnp
        import numpy as np
        E = 8
        K = 2
        D = 128
        H = 342
        B, S = (2, 256)

        def _moe_forward(x, centroid, Wg, bg, W1, b1, W2, b2):
            T = x.shape[0] * x.shape[1]
            xs = x.reshape(T, D)
            d2 = jnp.sum(xs * xs, axis=-1, keepdims=True) + jnp.sum(centroid * centroid, axis=-1)[None, :] - 2.0 * (xs @ centroid.T)
            dist = jnp.sqrt(jnp.maximum(d2, 1e-12))
            w, sel = jax.lax.top_k(dist, K)
            w = jax.nn.softmax(w.astype(jnp.float32), axis=1).astype(x.dtype)
            we = jnp.zeros((T, E), dtype=x.dtype).at[jnp.arange(T)[:, None], sel].add(w)
            out = jnp.zeros_like(xs)
            for e in range(E):
                h = jax.nn.silu(xs @ Wg[e] + bg[e]) * (xs @ W1[e] + b1[e])
                out = out + we[:, e:e + 1] * (h @ W2[e] + b2[e])
            return out.reshape(x.shape)
        return _moe_forward(x, centroid, Wg, bg, W1, b1, W2, b2)
    x = x + _L0_xattn_ref(ctx_768, _layernorm(x, axis=-1), mask_BxS2_bk0, L0_xattn_ln_x_g, L0_xattn_ln_x_b, L0_xattn_ln_l_g, L0_xattn_ln_l_b, L0_xattn_qn_g, L0_xattn_kn_g, L0_xattn_Wq, L0_xattn_Wkv, L0_xattn_Wlkv, L0_xattn_Wo, L0_xattn_bo)
    x = x + _L0_ffn_ref(_layernorm(x, axis=-1), L0_ffn_centroid, L0_ffn_Wg, L0_ffn_bg, L0_ffn_W1, L0_ffn_b1, L0_ffn_W2, L0_ffn_b2)
    return x

_drawn_inputs = setup_inputs


def setup_inputs(seed=0):
    import zlib

    import numpy as np

    out = dict(_drawn_inputs(seed))
    spreads = {'L0_xattn_ln_x_g': (1.0, 0.2),
     'L0_xattn_ln_x_b': (0.0, 0.31),
     'L0_xattn_ln_l_g': (1.0, 0.2),
     'L0_xattn_ln_l_b': (0.0, 0.1),
     'L0_xattn_qn_g': (1.0, 0.6),
     'L0_xattn_kn_g': (1.0, 0.6),
     'L0_xattn_bo': (0.0, 0.1),
     'L0_ffn_bg': (0.0, 0.8),
     'L0_ffn_b1': (0.0, 0.8),
     'L0_ffn_b2': (0.0, 0.484)}
    factors = {'L0_ffn_Wg': 7.526, 'L0_ffn_W1': 7.529, 'L0_ffn_W2': 6.812}
    for name, (base, spread) in spreads.items():
        noise = np.random.default_rng([zlib.crc32(name.encode()), seed]).standard_normal(out[name].shape)
        drawn = base * np.exp(spread * noise) if base else spread * noise
        out[name] = jnp.asarray(drawn.astype(out[name].dtype))
    for name, factor in factors.items():
        out[name] = (out[name] * factor).astype(out[name].dtype)
    return out
```

```python
from contextlib import ExitStack

import numpy as np

import concourse.bass as bass
from concourse import mybir

ALU = mybir.AluOpType
ACT = mybir.ActivationFunctionType
AX = mybir.AxisListType
F32 = mybir.dt.float32
F32R = mybir.dt.float32r
BF16 = mybir.dt.bfloat16
U8 = mybir.dt.uint8
I32 = mybir.dt.int32
U32 = mybir.dt.uint32

P = 128
B, S, D = 8, 256, 128
M, C = 512, 96
H, DH = 2, 64
QT, CT = S // P, M // P
KT = CT + QT
NK = KT * P
UNITS = QT * H
E, HID, HC = 8, 342, 3
HP = HID // HC
TOP = 2
ROW = D + 2
REGION = B * S + P
RING = 6
TILES = B * S * TOP // P + E - 1
FIRST = RING + (TILES - 1) % RING
SPARE = E
NOWHERE = 1 << 20
LN_EPS = 1e-5
RMS_FLOOR = 1e-16
BIG = 1e30
T_IOTA, T_BASE, T_TRI, T_TILE, T_FILL, TAB = np.cumsum([0, E, E, E * E, TILES, B * S // P]).tolist()
COLS = ["ln_x_g", "ln_x_b", "ln_l_g", "ln_l_b", "qn_g", "kn_g"]


def lin(b, per, k):
    if isinstance(b, int):
        return per * b + k
    i, c, n = b
    return i * (n * per) + (per * c + k)


def after(b, d):
    return b + d if isinstance(b, int) else (b[0], b[1] + d, b[2])


def mod(b, m):
    return b % m if isinstance(b, int) else b[1] % m


def part_of(b, m, per, k):
    if isinstance(b, int):
        return per * (b // m) + k
    i, c, n = b
    return i * (n // m * per) + (per * (c // m) + k)


def par(b):
    return mod(b, 2)


def wait(eng, sem, value):
    if isinstance(value, int) and value <= 0:
        return
    eng.wait_ge(sem, value)


def build(nc, a, out):
    with ExitStack() as ctx:
        def sb(name, shape, dt=F32):
            return ctx.enter_context(nc.sbuf_tensor(name, shape, dt))

        def bank(name, shape):
            return ctx.enter_context(nc.psum_tensor(name, shape, F32))

        def sem(name):
            return ctx.enter_context(nc.semaphore(name))

        xs = [sb(f"xs{p}", [P, QT, D]) for p in range(2)]
        cs = [sb(f"cs{p}", [P, CT, C]) for p in range(2)]
        xb = sb("xb", [P, (B + 1) * QT, D])
        mask_u8 = sb("mask_u8", [P, (B + 1) * M], U8)
        mbias = [sb(f"mbias{p}", [P, NK]) for p in range(2)]
        wqkv_l = sb("wqkv_l", [P, 3 * D])
        wkv_c = sb("wkv_c", [C, 2 * D])
        wo = sb("wo", [P, D])
        cols = sb("cols", [P, len(COLS)])
        gqk = sb("gqk", [P, 1])
        bo_b = sb("bo_b", [P, D])
        eye = sb("eye", [P, P])
        neghalf = sb("neghalf", [P, 16])
        stat = sb("stat", [P, CT + QT, 6])
        mv = sb("mv", [P, CT + QT, 2])
        stat2 = sb("stat2", [P, QT, 6])
        mv2 = sb("mv2", [P, QT, 2])
        var = sb("var", [P, CT + QT])
        rstd = sb("rstd", [P, CT + QT])
        var2 = sb("var2", [P, QT])
        rstd2 = sb("rstd2", [P, QT])
        xhat = sb("xhat", [P, QT, D])
        xz = sb("xz", [P, 2, QT, D])
        cn = sb("cn", [P, 2, CT, C])
        lnT = sb("lnT", [P, S])
        cT = sb("cT", [C, M])
        kvq = [sb(f"kvq{p}", [P, KT, 3 * D]) for p in range(2)]
        sq = sb("sq", [P, KT + QT, D])
        ss = sb("ss", [P, (KT + QT) * H])
        ssf = sb("ssf", [P, (KT + QT) * H])
        rms = sb("rms", [P, (KT + QT) * H])
        nrq = sb("nrq", [P, 2, QT * H])
        kn = sb("kn", [P, KT, D])
        qT = [sb(f"qT{p}", [P, S]) for p in range(2)]
        kT = [sb(f"kT{p}", [P, NK]) for p in range(2)]
        sm = [sb(f"sm{p}", [P, NK]) for p in range(2)]
        negmax = sb("negmax", [P, 2])
        prob = [sb(f"prob{p}", [P, NK]) for p in range(2)]
        den = sb("den", [P, 2])
        rden = sb("rden", [P, 2])
        pT = [sb(f"pT{p}", [P, NK]) for p in range(2)]
        o_sb = sb("o_sb", [P, QT, D])
        oT = sb("oT", [P, S])
        x2 = xb
        stat3 = sb("stat3", [P, QT, 6])
        mv3 = sb("mv3", [P, QT, 2])
        var3 = sb("var3", [P, QT])
        rstd3 = sb("rstd3", [P, QT])
        rows_out = [sb(f"rows_out{p}", [P, QT, TOP, ROW]) for p in range(2)]
        xfT = sb("xfT", [P, S])
        square_scrap = sb("square_scrap", [P, QT, D], BF16)
        xx = sb("xx", [P, QT])
        cenT = sb("cenT", [P, E])
        cen2 = sb("cen2", [P, E])
        cc = sb("cc", [P, E])
        d2raw = sb("d2raw", [P, QT, E])
        d2 = sb("d2", [P, QT, E])
        best = sb("best", [P, QT, 8])
        choice = sb("choice", [P, QT, 8], U32)
        dist = sb("dist", [P, QT, TOP])
        dgap = sb("dgap", [P, QT])
        egap = sb("egap", [P, QT])
        esum = sb("esum", [P, QT])
        onehot = sb("onehot", [P, QT, TOP, E])
        picks = sb("picks", [P, QT, E], BF16)
        before = sb("before", [P, E])
        before_b = sb("before_b", [P, E], BF16)
        before_t = sb("before_t", [P, E])
        ranks = sb("ranks", [P, QT, E])
        ranked = sb("ranked", [P, QT, TOP, E])
        pos_f = sb("pos_f", [P, QT * TOP])
        pos = [sb(f"pos{p}", [P, QT * TOP], U32) for p in range(2)]
        tab = sb("tab", [P, TAB])
        slot_tab = sb("slot_tab", [P, (B + 1) * QT, TOP], I32)
        triu_f = sb("triu_f", [P, P])
        triu = sb("triu", [P, P], BF16)
        ones_f = sb("ones_f", [P, P])
        ones = sb("ones", [P, P], BF16)
        half_ = sb("half_", [P, QT * TOP])
        pad_row = sb("pad_row", [P, ROW])
        counts = sb("counts", [P, E])
        fills = sb("fills", [P, E, B * S // P])
        ntiles = sb("ntiles", [P, E])
        cum_terms = sb("cum_terms", [P, E, E])
        cum = sb("cum", [P, E])
        passed = sm[0][:, 0:TILES * E].rearrange("p (t e) -> p t e", e=E)
        expert = sb("expert", [P, TILES])
        start_terms = sm[1][:, 0:TILES * E].rearrange("p (t e) -> p t e", e=E)
        start = sb("start", [P, TILES])
        since = sb("since", [P, TILES])
        row_at = sb("row_at", [P, TILES], I32)
        expert_at = sb("expert_at", [P, TILES], I32)
        pad_at = sb("pad_at", [P, E], I32)
        w1_in = sb("w1_in", [P, 2 * HID])
        w2_in = sb("w2_in", [HP, HC * D])
        w1_hi = sb("w1_hi", [P, E, 2 * HID], F32R)
        w1_lo = sb("w1_lo", [P, E, 2 * HID], F32R)
        w2_hi = sb("w2_hi", [HP, E, HC * D], F32R)
        w2_lo = sb("w2_lo", [HP, E, HC * D], F32R)
        BW = 2 * HID + D
        bias_in = sb("bias_in", [E, BW])
        bias_rest = sb("bias_rest", [E, BW])
        bias_part = [sb(f"bias_part{i}", [E, BW], BF16) for i in range(3)]
        bias = sb("bias", [3, E, BW], BF16)
        xT_hi = [sb(f"xT_hi{i}", [P, P], F32R) for i in range(2)]
        xT_lo = [sb(f"xT_lo{i}", [P, P], F32R) for i in range(2)]
        gate = [pT[i][:, 0:HID] for i in range(2)]
        hid = [prob[i][:, 0:HID] for i in range(2)]
        hT_hi = [sb(f"hT_hi{i}", [HP, HC * P], F32R) for i in range(2)]
        hT_lo = [sb(f"hT_lo{i}", [HP, HC * P], F32R) for i in range(2)]
        done = [kvq[i][:].rearrange("p t n -> p (t n)") for i in range(2)]
        xt = [done[0][:, i * ROW:(i + 1) * ROW] for i in range(RING)]
        y = [done[1][:, i * D:(i + 1) * D] for i in range(RING)]
        y_in = [done[i][:, 0:8 * D].rearrange("p (t k d) -> p t k d", k=TOP, d=D) for i in range(2)]
        y_sum = [done[i][:, 8 * D:12 * D].rearrange("p (t d) -> p t d", d=D) for i in range(2)]
        out_sb = [done[i][:, 12 * D:16 * D].rearrange("p (t d) -> p t d", d=D) for i in range(2)]

        S_ps = bank("S_ps", [P, 1024])
        Ta = bank("Ta", [P, 512])
        Tb = bank("Tb", [P, 512])
        O_ps = bank("O_ps", [P, 512])
        M0 = bank("M0", [P, 512])
        M1 = bank("M1", [P, 512])
        X_ps = bank("X_ps", [P, 512])

        G_ps = [S_ps[:, 0:HID], S_ps[:, 512:512 + HID]]
        U_ps = [Ta[:, 0:HID], Tb[:, 0:HID]]
        HT_ps, Y_ps, XT_ps = M0, O_ps, M1

        sorted_rows = nc.dram_tensor("sorted_rows", (E * REGION + SPARE * P, ROW), F32).ap()
        results = nc.dram_tensor("results", (B * S * TOP, D), F32).ap()

        ld_const = sem("ld_const")
        rows_in = [sem(f"rows_in{p}") for p in range(2)]
        zeroed = sem("zeroed")
        masked = sem("masked")
        gqk_done = sem("gqk_done")
        stat1_done = sem("stat1_done")
        rstd1_done = sem("rstd1_done")
        norm1_done = sem("norm1_done")
        stat2_done = sem("stat2_done")
        rstd2_done = sem("rstd2_done")
        xz_done = sem("xz_done")
        xb_done = sem("xb_done")
        prep_pe = sem("prep_pe")
        m0_out = sem("m0_out")
        m1_out = sem("m1_out")
        sq_done = sem("sq_done")
        ss_done = sem("ss_done")
        floor_done = sem("floor_done")
        rms_done = sem("rms_done")
        knl_done = sem("knl_done")
        knc_done = sem("knc_done")
        scores_ready = sem("scores_ready")
        masked_max = sem("masked_max")
        prob_ready = sem("prob_ready")
        ta_ready = sem("ta_ready")
        tb_ready = sem("tb_ready")
        pa_ready = sem("pa_ready")
        pb_ready = sem("pb_ready")
        pv_done = sem("pv_done")
        rden_done = sem("rden_done")
        o_ready = sem("o_ready")
        post_pe = sem("post_pe")
        oT_ready = sem("oT_ready")
        x2_ready = sem("x2_ready")
        stat3_done = sem("stat3_done")
        rstd3_done = sem("rstd3_done")
        xf_done = sem("xf_done")
        xfT_ready = sem("xfT_ready")
        xx_done = sem("xx_done")
        router_done = sem("router_done")
        dist_done = sem("dist_done")
        egap_done = sem("egap_done")
        weight_done = sem("weight_done")
        slot_done = sem("slot_done")
        x_free = sem("x_free")
        pos_done = sem("pos_done")
        before_done = sem("before_done")
        scattered = [sem(f"scattered{p}") for p in range(2)]
        w_in = sem("w_in")
        w_hi = sem("w_hi")
        w_lo = sem("w_lo")
        bias_ld = sem("bias_ld")
        bias_chain = sem("bias_chain")
        bias_set = sem("bias_set")
        setup_v = sem("setup_v")
        setup_t = sem("setup_t")
        counted = sem("counted")
        table = sem("table")
        padded = sem("padded")
        xt_in = [sem(f"xt_in{i}") for i in range(RING)]
        y_out = [sem(f"y_out{i}") for i in range(RING)]
        xT_pe = sem("xT_pe")
        xT_hi_set = sem("xT_hi_set")
        xT_lo_set = sem("xT_lo_set")
        gu_pe = sem("gu_pe")
        gate_set = sem("gate_set")
        hid_set = sem("hid_set")
        hT_pe = sem("hT_pe")
        hT_hi_set = sem("hT_hi_set")
        hT_lo_set = sem("hT_lo_set")
        y_pe = sem("y_pe")
        y_set = sem("y_set")
        y_back = [sem(f"y_back{i}") for i in range(2)]
        y_summed = sem("y_summed")
        out_set = sem("out_set")
        stored = [sem(f"stored{i}") for i in range(2)]

        col = {n: cols[:, i:i + 1] for i, n in enumerate(COLS)}
        x_v = a["x"].rearrange("(t p) d -> p t d", p=P)
        c_v = a["ctx"].rearrange("(t p) d -> p t d", p=P)
        out_v = out.rearrange("(t p) d -> p t d", p=P)
        w1_v = a["w1"].rearrange("p (e n) -> p e n", e=E)
        w2_v = a["w2"].rearrange("p (e n) -> p e n", e=E)
        res_v = results.rearrange("(t p k) d -> p t k d", p=P, k=TOP)
        TABLE_STEPS = 11
        LOADED = 16 * 11

        block = ctx.enter_context(nc.Block())

        def held(eng, *waits):
            values = [v if isinstance(v, int) else eng.to_reg(v) for _, v in waits]
            eng.wait_ge(zeroed, 1)
            for (s, _), v in zip(waits, values):
                wait(eng, s, v)

        def load_rows(sp, n):
            q = par(n)
            if not isinstance(n, int):
                held(sp, (norm1_done, lin(n, 2, 2 - 4)),
                         (xb_done, lin(n, 1, 1 - 2)))
            sp.dma_start(xs[q][:], x_v[:, bass.ds(lin(n, QT, 0), QT), :]).then_inc(rows_in[q], 16)
            sp.dma_start(cs[q][:], c_v[:, bass.ds(lin(n, CT, 0), CT), :]).then_inc(rows_in[q], 16)

        def load_weights(sp, e):
            held(sp, (w_hi, lin(e, 1, 0)),
                     (w_lo, lin(e, 1, 0)))
            sp.dma_start(w1_in[:], w1_v[:, bass.ds(lin(e, 1, 0), 1), :]).then_inc(w_in, 16)
            sp.dma_start(w2_in[:], w2_v[:, bass.ds(lin(e, 1, 0), 1), :]).then_inc(w_in, 16)

        def tiles(eng, step):
            for t in range(FIRST):
                step(t)
            with eng.Fori(0, (TILES - 1 - FIRST) // RING) as i:
                for c in range(RING):
                    step((i, FIRST + c, RING))
            step(TILES - 1)

        @block.sync
        def _(sp):
            load_rows(sp, 0)
            for t, n in ((cols, "cols"), (eye, "eye"), (wqkv_l, "wqkv_l"), (wkv_c, "wkv_c")):
                sp.dma_start(t[:], a[n]).then_inc(ld_const, 16)
            sp.dma_start(mask_u8[:, 0:B * M], a["mask"].rearrange("b m -> (b m)").partition_broadcast(P)).then_inc(ld_const, 16)
            sp.dma_start(wo[:], a["wo"]).then_inc(ld_const, 16)
            sp.dma_start(bo_b[:], a["bo"].partition_broadcast(P)).then_inc(ld_const, 16)
            sp.dma_start(tab[:], a["tab"]).then_inc(ld_const, 16)
            sp.dma_start(slot_tab[:, 0:B * QT, :], a["slot_tab"]).then_inc(ld_const, 16)
            sp.dma_start(triu_f[:], a["triu"]).then_inc(ld_const, 16)
            sp.dma_start(cenT[:], a["cenT"]).then_inc(ld_const, 16)
            load_rows(sp, 1)
            sp.dma_start(bias_in[:], a["bias"]).then_inc(bias_ld, 16)
            load_weights(sp, 0)
            sp.wait_ge(bias_chain, 5)
            for j in range(3):
                sp.dma_start(bias[j:j + 1, :, :], bias_part[j][:]).then_inc(bias_set, 16)
            with sp.Fori(0, 3) as i:
                for c in (2, 3):
                    load_rows(sp, (i, c, 2))
                    load_weights(sp, (i, c - 1, 2))
            sp.wait_ge(rows_in[0], 32 * B // 2)
            sp.sem_inc(rows_in[0], 32)
            load_weights(sp, E - 1)
            sp.wait_ge(table, TABLE_STEPS + 1)
            for e in range(E):
                row = sp.value_load(pad_at[0:1, e:e + 1], min_val=0, max_val=E * REGION - P)
                sp.dma_start(sorted_rows[bass.ds(row, P), :], pad_row[:]).then_inc(padded, 16)
            for q in range(2):
                sp.wait_ge(scattered[q], 64 + 64 * B // 2)
            sp.wait_ge(padded, 16 * E)

            def load_tile(t):
                q = mod(t, RING)
                held(sp, (y_out[q], part_of(t, RING, 16, 0)))
                row = sp.value_load(row_at[0:1, bass.ds(lin(t, 1, 0), 1)], min_val=0, max_val=(E * REGION + SPARE * P) - P)
                sp.dma_start(xt[q], sorted_rows[bass.ds(row, P), :]).then_inc(xt_in[q], 16)

            tiles(sp, load_tile)
            for q in range(RING):
                sp.wait_ge(y_out[q], 16 * len(range(q, TILES, RING)))
            for j in range(4):
                if j >= 2:
                    sp.wait_ge(out_set, j - 1)
                sp.dma_start(y_in[j % 2], res_v[:, 4 * j:4 * j + 4, :, :]).then_inc(y_back[j % 2], 16)
            for j in range(4):
                sp.wait_ge(out_set, j + 1)
                sp.dma_start(out_v[:, 4 * j:4 * j + 4, :], out_sb[j % 2]).then_inc(stored[j % 2], 16)
            for q in range(2):
                sp.wait_ge(stored[q], 16 * 2)

        def pool_pow(p, out_, in_, power):
            return nc.gpsimd.tensor_tensor(out_, in_, power, ALU.pow)

        def pool_rstd(p, n, var_, rstd_, mean_var, stats, own):
            held(p, (stats, lin(n, 2, 2)))
            nc.gpsimd.tensor_scalar(var_, mean_var[:, :, 1], LN_EPS, None, ALU.add).then_inc(own, 1)
            wait(p, own, lin(n, 2, 1))
            w = mean_var.shape[1]
            nc.gpsimd.tensor_tensor(rstd_, var_, neghalf[:, 0:w], ALU.pow).then_inc(own, 1)

        def pool_rstd1(p, n):
            pool_rstd(p, n, var[:], rstd[:], mv, stat1_done, rstd1_done)

        def pool_rstd2(p, n):
            pool_rstd(p, n, var2[:], rstd2[:], mv2, stat2_done, rstd2_done)

        def pool_rstd3(p, m):
            pool_rstd(p, m, var3[:], rstd3[:], mv3, stat3_done, rstd3_done)

        def pool_xb(p, n):
            q = par(n)
            held(p, (rows_in[q], part_of(n, 2, 32, 32)))
            nc.gpsimd.tensor_tensor(xb[:, bass.ds(lin(n, QT, 0), QT), :], xs[q][:],
                                    bo_b[:].unsqueeze(1).to_broadcast([P, QT, D]), ALU.add).then_inc(xb_done, 1)

        def pool_router(p, m):
            q = par(m)
            held(p, (scattered[q], part_of(m, 2, 64, 64)))
            nc.gpsimd.tensor_copy(rows_out[q][:].bitcast(I32)[:, :, :, D + 1],
                                  slot_tab[:, bass.ds(lin(m, QT, 0), QT), :]).then_inc(slot_done, 1)
            wait(p, router_done, lin(m, 6, 3))
            nc.gpsimd.tensor_tensor(dist[:], best[:, :, 0:TOP], half_[:].rearrange("p (t k) -> p t k", k=TOP),
                                    ALU.pow).then_inc(dist_done, 1)
            wait(p, dist_done, lin(m, 2, 1))
            nc.gpsimd.tensor_tensor(dgap[:], dist[:, :, 1], dist[:, :, 0], ALU.subtract).then_inc(dist_done, 1)

        def pool_scatter(p, m):
            q = par(m)
            held(p, (pos_done, lin(m, 3, 3)),
                    (weight_done, lin(m, 3, 3)),
                    (slot_done, lin(m, 1, 1)))
            for t in range(QT):
                for k in range(TOP):
                    nc.gpsimd.indirect_dma_start(
                        out=sorted_rows[:, :],
                        out_offset=bass.IndirectOffsetOnAxis(ap=pos[q][:, TOP * t + k:TOP * t + k + 1], axis=0),
                        in_=rows_out[q][:, t, k, :], in_offset=None).then_inc(scattered[q], 16)

        def unit_keys(eng, q, t0, t1):
            return eng.tensor_tensor(
                kn[:, t0:t1, :].rearrange("p t (h d) -> p t h d", h=H),
                kvq[q][:, t0:t1, 0:D].rearrange("p t (h d) -> p t h d", h=H),
                rms[:, t0 * H:t1 * H].rearrange("p (t h) -> p t h", h=H).unsqueeze(3).to_broadcast([P, t1 - t0, H, DH]),
                ALU.mult)

        def pool_rms(p, n, part):
            q = par(n)
            c0, c1 = ((CT * H, (KT + QT) * H), (0, CT * H))[part]
            held(p, (ss_done, lin(n, 2, part + 1)))
            nc.gpsimd.tensor_scalar(ssf[:, c0:c1], ss[:, c0:c1], 1.0 / DH, RMS_FLOOR,
                                    ALU.mult, ALU.max).then_inc(floor_done, 1)
            wait(p, floor_done, lin(n, 2, part + 1))
            nc.gpsimd.tensor_tensor(rms[:, c0:c1], ssf[:, c0:c1], neghalf[:, 0:c1 - c0],
                                    ALU.pow).then_inc(rms_done, 1)
            if part == 0:
                held(p, (rms_done, lin(n, 2, 1)),
                        (masked_max, lin(n, UNITS, -UNITS)))
                nc.gpsimd.tensor_scalar(nrq[:, q, :], rms[:, KT * H:(KT + QT) * H], -float(DH) ** -0.5, None, ALU.mult)
                wait(p, prep_pe, lin(n, 8, -1))
                unit_keys(nc.gpsimd, q, CT, KT).then_inc(knl_done, 1)

        def pool_body(p, b, first=False, last=False, ahead=True):
            n, m, f = after(b, 1), after(b, -1), after(b, 2)
            if ahead:
                pool_rstd1(p, f)
            if not last:
                pool_rms(p, n, 0)
            if not first:
                pool_rstd3(p, m)
            if ahead:
                pool_rstd2(p, f)
            if not last:
                pool_rms(p, n, 1)
            if ahead:
                pool_xb(p, f)
            if not first:
                pool_router(p, m)
                pool_scatter(p, m)

        @block.gpsimd
        def _(p):
            nc.gpsimd.memset(neghalf[:], -0.5).then_inc(zeroed, 1)
            p.wait_ge(zeroed, 1)
            p.sem_inc(y_set, 1)
            nc.gpsimd.memset(half_[:], 0.5)
            nc.gpsimd.memset(ones_f[:], 1.0)
            nc.gpsimd.memset(ones[:], 1.0)
            nc.gpsimd.memset(before[:], 0.0)
            nc.gpsimd.memset(before_b[:], 0.0)
            nc.gpsimd.memset(pad_row[:, 0:D + 1], 0.0)
            nc.gpsimd.memset(pad_row[:].bitcast(I32)[:, D + 1:ROW], NOWHERE)
            nc.gpsimd.memset(mask_u8[:, B * M:], 0)
            for q in range(2):
                ins = nc.gpsimd.memset(mbias[q][:, M:NK], 0.0)
            ins.then_inc(zeroed, 1)
            pool_rstd1(p, 0)
            pool_rstd2(p, 0)
            p.wait_ge(zeroed, 2)
            for j in range(SPARE):
                p.dma_start(sorted_rows[E * REGION + j * P:E * REGION + (j + 1) * P, :], pad_row[:]).then_inc(scattered[j % 2], 16)
            p.wait_ge(ld_const, LOADED)
            pool_xb(p, 0)
            pool_rms(p, 0, 0)
            pool_rms(p, 0, 1)
            pool_rstd1(p, 1)
            pool_rstd2(p, 1)
            pool_xb(p, 1)
            p.wait_ge(bias_ld, 16)
            nc.gpsimd.tensor_copy(bias_part[0][:], bias_in[:]).then_inc(bias_chain, 1)
            p.wait_ge(bias_chain, 1)
            nc.gpsimd.tensor_tensor(bias_rest[:], bias_in[:], bias_part[0][:], ALU.subtract).then_inc(bias_chain, 1)
            p.wait_ge(bias_chain, 2)
            nc.gpsimd.tensor_copy(bias_part[1][:], bias_rest[:]).then_inc(bias_chain, 1)
            p.wait_ge(bias_chain, 3)
            nc.gpsimd.tensor_tensor(bias_in[:], bias_rest[:], bias_part[1][:], ALU.subtract).then_inc(bias_chain, 1)
            p.wait_ge(bias_chain, 4)
            nc.gpsimd.tensor_copy(bias_part[2][:], bias_in[:]).then_inc(bias_chain, 1)
            pool_body(p, 0, first=True)
            with p.Fori(0, 3) as i:
                pool_body(p, (i, 1, 2))
                pool_body(p, (i, 2, 2))
            pool_body(p, 7, last=True, ahead=False)
            pool_rstd3(p, 7)
            pool_router(p, 7)
            pool_scatter(p, 7)

            def send(t):
                q = mod(t, RING)
                held(p, (y_set, lin(t, 1, 2)))
                nc.gpsimd.indirect_dma_start(
                    out=results[:, :],
                    out_offset=bass.IndirectOffsetOnAxis(ap=xt[q].bitcast(U32)[:, D + 1:ROW], axis=0),
                    in_=y[q], in_offset=None, bounds_check=B * S * TOP - 1, oob_is_err=False).then_inc(y_out[q], 16)

            tiles(p, send)
            for j in range(4):
                p.wait_ge(y_back[j % 2], 16 * (j // 2 + 1))
                if j >= 2:
                    p.wait_ge(out_set, j - 1)
                nc.gpsimd.tensor_tensor(y_sum[j % 2], y_in[j % 2][:, :, 0, :], y_in[j % 2][:, :, 1, :],
                                        ALU.add).then_inc(y_summed, 1)

        def dve_stats(v, n):
            wait(v, rows_in[par(n)], part_of(n, 2, 32, 32))
            wait(v, norm1_done, lin(n, 2, 0))
            for t in range(QT):
                nc.vector.bn_stats(stat[:, CT + t, :], xs[par(n)][:, t, :])
            for t in range(CT):
                ins = nc.vector.bn_stats(stat[:, t, :], cs[par(n)][:, t, :])
            ins.then_inc(stat1_done, 1)
            held(v, (stat1_done, lin(n, 2, 1)))
            for t in range(CT + QT):
                ins = nc.vector.bn_aggr(mv[:, t, :], stat[:, t, :])
            ins.then_inc(stat1_done, 1)

        def dve_stats2(v, n):
            wait(v, norm1_done, lin(n, 2, 1))
            wait(v, xz_done, lin(n, 1, 0))
            for t in range(QT):
                ins = nc.vector.bn_stats(stat2[:, t, :], xhat[:, t, :])
            ins.then_inc(stat2_done, 1)
            held(v, (stat2_done, lin(n, 2, 1)))
            for t in range(QT):
                ins = nc.vector.bn_aggr(mv2[:, t, :], stat2[:, t, :])
            ins.then_inc(stat2_done, 1)

        def dve_norm1(v, n):
            q = par(n)
            wait(v, rstd1_done, lin(n, 2, 2))
            wait(v, xz_done, lin(n, 1, 0))
            for t in range(QT):
                ins = nc.vector.tensor_scalar(xhat[:, t, :], xs[q][:, t, :], mv[:, CT + t, 0:1],
                                              rstd[:, CT + t:CT + t + 1], ALU.subtract, ALU.mult)
            ins.then_inc(norm1_done, 1)
            wait(v, prep_pe, lin(n, 8, 2 - 16))
            for t in range(CT):
                ins = nc.vector.tensor_scalar(cn[:, q, t, :], cs[q][:, t, :], mv[:, t, 0:1],
                                              rstd[:, t:t + 1], ALU.subtract, ALU.mult)
            ins.then_inc(norm1_done, 1)

        def dve_xz(v, n):
            q = par(n)
            wait(v, rstd2_done, lin(n, 2, 2))
            wait(v, prep_pe, lin(n, 8, 1 - 16))
            for t in range(QT):
                ins = nc.vector.tensor_scalar(xz[:, q, t, :], xhat[:, t, :], mv2[:, t, 0:1],
                                              rstd2[:, t:t + 1], ALU.subtract, ALU.mult)
            ins.then_inc(xz_done, 1)

        def dve_prep(v, n, step):
            q = par(n)
            wait(v, prep_pe, lin(n, 8, step + 1))
            if step == 1:
                wait(v, prep_pe, lin(n, 8, 6 - 8))
                ins = nc.vector.tensor_scalar(cT[:], M1[0:C, :], col["ln_x_g"][0:C], col["ln_x_b"][0:C], ALU.mult, ALU.add)
            if step == 3:
                wait(v, pv_done, lin(n, UNITS, -UNITS))
                ins = nc.vector.tensor_copy(kvq[q][:, CT + 1, :], M1[:, 0:3 * D])
            if step == 5:
                ins = nc.vector.tensor_copy(kvq[q][:, 2:4, 0:2 * D], M1[:].rearrange("p (t n) -> p t n", t=2))
            if step == 7:
                wait(v, scores_ready, lin(n, UNITS, -UNITS))
                ins = nc.vector.tensor_copy(kT[q][:, 0:M], M1[:])
            ins.then_inc(m1_out, 1)

        def dve_ss(v, n, part):
            wait(v, sq_done, lin(n, 2, part + 1))
            wait(v, rms_done, lin(n, 2, part + 1 - 2))
            t0, t1 = ((CT, KT + QT), (0, CT))[part]
            nc.vector.tensor_reduce(ss[:, t0 * H:t1 * H], sq[:, t0:t1, :].rearrange("p t (h d) -> p (t h) d", h=H),
                                    AX.X, ALU.add).then_inc(ss_done, 1)

        def dve_keys(v, n):
            wait(v, rms_done, lin(n, 2, 2))
            wait(v, prep_pe, lin(n, 8, 0))
            unit_keys(nc.vector, par(n), 0, CT).then_inc(knc_done, 1)

        def dve_max(v, b, u):
            q = u % 2
            if u == 0:
                wait(v, knl_done, lin(b, 1, 1))
                wait(v, masked, lin(b, 1, 1))
                v.wait_ge(zeroed, 2)
            held(v, (scores_ready, lin(b, UNITS, u + 1)),
                    (prob_ready, lin(b, UNITS, u + 1 - 2)))
            nc.vector.tensor_tensor_reduce(out=sm[q][:], in0=S_ps[:, 0:NK],
                                           in1=mbias[par(b)][:],
                                           scale=nrq[:, par(b), u:u + 1], scalar=3e38, op0=ALU.add, op1=ALU.min,
                                           accum_out=negmax[:, q:q + 1]).then_inc(masked_max, 1)

        def dve_o(v, b, u):
            q, (t, h) = u % 2, divmod(u, H)
            wait(v, prob_ready, lin(b, UNITS, u + 1))
            nc.vector.reciprocal(rden[:, q:q + 1], den[:, q:q + 1]).then_inc(rden_done, 1)
            wait(v, rden_done, lin(b, UNITS, u + 1))
            wait(v, pv_done, lin(b, UNITS, u + 1))
            if u == 0:
                wait(v, post_pe, lin(b, 2, 1 - 2))
            nc.vector.tensor_scalar(o_sb[:, t, h * DH:(h + 1) * DH], O_ps[:, 0:DH], rden[:, q:q + 1], None,
                                    ALU.mult).then_inc(o_ready, 1)

        def dve_x2(v, m):
            wait(v, post_pe, lin(m, 5, 2))
            wait(v, xb_done, lin(m, 1, 1))
            rows = x2[:, bass.ds(lin(m, QT, 0), QT), :]
            nc.vector.tensor_tensor(rows, X_ps[:, 0:S].rearrange("p (t d) -> p t d", t=QT),
                                    xb[:, bass.ds(lin(m, QT, 0), QT), :], ALU.add).then_inc(x2_ready, 1)
            held(v, (x2_ready, lin(m, 1, 1)))
            for t in range(QT):
                ins = nc.vector.bn_stats(stat3[:, t, :], x2[:, bass.ds(lin(m, QT, t), 1), :].rearrange("p o d -> p (o d)"))
            ins.then_inc(stat3_done, 1)
            held(v, (stat3_done, lin(m, 2, 1)))
            for t in range(QT):
                ins = nc.vector.bn_aggr(mv3[:, t, :], stat3[:, t, :])
            ins.then_inc(stat3_done, 1)

        def dve_xf(v, m):
            q = par(m)
            wait(v, rstd3_done, lin(m, 2, 2))
            wait(v, scattered[q], part_of(m, 2, 64, 64))
            for t in range(QT):
                ins = nc.vector.tensor_scalar(
                    rows_out[q][:, t, :, 0:D],
                    x2[:, bass.ds(lin(m, QT, t), 1), :].to_broadcast([P, TOP, D]),
                    mv3[:, t, 0:1], rstd3[:, t:t + 1], ALU.subtract, ALU.mult)
            ins.then_inc(xf_done, 1)

        def dve_top(v, m):
            wait(v, post_pe, lin(m, 5, 4))
            if m == 0:
                v.wait_ge(x_free, 1)
            nc.vector.scalar_tensor_tensor(out=d2raw[:], in0=X_ps[:, 0:QT * E].rearrange("p (t e) -> p t e", t=QT),
                                           scalar=-2.0, in1=cc[:].unsqueeze(1).to_broadcast([P, QT, E]),
                                           op0=ALU.mult, op1=ALU.add).then_inc(router_done, 1)
            held(v, (router_done, lin(m, 6, 1)), (xx_done, lin(m, 1, 1)))
            for t in range(QT):
                ins = nc.vector.tensor_scalar(d2[:, t, :], d2raw[:, t, :], xx[:, t:t + 1], 1e-12, ALU.add, ALU.max)
            ins.then_inc(router_done, 1)
            held(v, (router_done, lin(m, 6, 2)))
            for t in range(QT):
                ins = nc.vector.max(best[:, t, :], d2[:, t, :])
            ins.then_inc(router_done, 1)
            held(v, (router_done, lin(m, 6, 3)))
            for t in range(QT):
                ins = nc.vector.max_index(choice[:, t, :], best[:, t, :], d2[:, t, :])
            ins.then_inc(router_done, 1)
            wait(v, router_done, lin(m, 6, 4))
            nc.vector.tensor_tensor(onehot[:], tab[:, T_IOTA:T_IOTA + E].unsqueeze(1).unsqueeze(1).to_broadcast([P, QT, TOP, E]),
                                    choice[:, :, 0:TOP].unsqueeze(3).to_broadcast([P, QT, TOP, E]),
                                    ALU.is_equal).then_inc(router_done, 1)
            wait(v, router_done, lin(m, 6, 5))
            nc.vector.tensor_tensor(picks[:], onehot[:, :, 0, :], onehot[:, :, 1, :], ALU.add).then_inc(router_done, 1)

        def dve_place(v, m):
            q = par(m)
            wait(v, post_pe, lin(m, 5, 5))
            nc.vector.tensor_tensor(ranks[:], X_ps[:, 0:QT * E].rearrange("p (t e) -> p t e", t=QT),
                                    tab[:, T_BASE:T_BASE + E].unsqueeze(1).to_broadcast([P, QT, E]), ALU.add).then_inc(x_free, 1)
            wait(v, x_free, lin(m, 1, 2))
            nc.vector.tensor_tensor(ranked[:], onehot[:], ranks[:].unsqueeze(2).to_broadcast([P, QT, TOP, E]),
                                    ALU.mult).then_inc(pos_done, 1)
            wait(v, pos_done, lin(m, 3, 1))
            nc.vector.tensor_reduce(pos_f[:], ranked[:].rearrange("p t k e -> p (t k) e"), AX.X, ALU.add).then_inc(pos_done, 1)
            nc.vector.tensor_tensor(before_t[:], before[:], picks[:, 0, :], ALU.add).then_inc(before_done, 1)
            wait(v, before_done, lin(m, 3, 1))
            nc.vector.tensor_tensor(before[:], before_t[:], picks[:, 1, :], ALU.add).then_inc(before_done, 1)
            wait(v, before_done, lin(m, 3, 2))
            nc.vector.tensor_copy(before_b[:], before[:]).then_inc(before_done, 1)
            wait(v, pos_done, lin(m, 3, 2))
            wait(v, scattered[q], part_of(m, 2, 64, 64))
            nc.vector.tensor_copy(pos[q][:], pos_f[:]).then_inc(pos_done, 1)

        def dve_weight(v, m):
            q = par(m)
            wait(v, egap_done, lin(m, 1, 1))
            nc.vector.tensor_scalar(esum[:], egap[:], 1.0, None, ALU.add).then_inc(weight_done, 1)
            wait(v, weight_done, lin(m, 3, 1))
            nc.vector.reciprocal(rows_out[q][:, :, 0, D], esum[:]).then_inc(weight_done, 1)
            wait(v, weight_done, lin(m, 3, 2))
            nc.vector.tensor_tensor(rows_out[q][:, :, 1, D], egap[:], rows_out[q][:, :, 0, D], ALU.mult).then_inc(weight_done, 1)

        def dve_split(v, e):
            wait(v, w_hi, lin(e, 1, 1))
            nc.vector.tensor_tensor(w1_lo[:, bass.ds(lin(e, 1, 0), 1), :], w1_in[:].unsqueeze(1),
                                    w1_hi[:, bass.ds(lin(e, 1, 0), 1), :].bitcast(F32), ALU.subtract)
            nc.vector.tensor_tensor(w2_lo[:, bass.ds(lin(e, 1, 0), 1), :], w2_in[:].unsqueeze(1),
                                    w2_hi[:, bass.ds(lin(e, 1, 0), 1), :].bitcast(F32), ALU.subtract).then_inc(w_lo, 1)

        def dve_body(v, b, first=False, last=False, ahead=True):
            n, m, f = after(b, 1), after(b, -1), after(b, 2)
            dve_max(v, b, 1)
            if not last:
                dve_prep(v, n, 1)
            if ahead:
                dve_stats(v, f)
            dve_o(v, b, 0)
            if not last:
                dve_prep(v, n, 3)
            if not first:
                dve_x2(v, m)
            dve_max(v, b, 2)
            if not last:
                dve_ss(v, n, 0)
            dve_o(v, b, 1)
            if not last:
                dve_prep(v, n, 5)
            if ahead:
                dve_norm1(v, f)
                dve_stats2(v, f)
            if not first:
                dve_xf(v, m)
            dve_max(v, b, 3)
            if not last:
                dve_ss(v, n, 1)
            dve_o(v, b, 2)
            dve_split(v, b)
            if not last:
                dve_keys(v, n)
                dve_prep(v, n, 7)
            if not first:
                dve_top(v, m)
            if not last:
                dve_max(v, n, 0)
            if ahead:
                dve_xz(v, f)
            if not first:
                dve_place(v, m)
                dve_weight(v, m)
            dve_o(v, b, 3)

        def v_tile(xT_step, hid_step, hT_step, t):
            if t != TILES - 1:
                xT_step(after(t, 1))
            if t != 0:
                hT_step(after(t, -1))
            hid_step(t)

        @block.vector
        def _(v):
            dve_stats(v, 0)
            dve_norm1(v, 0)
            dve_stats2(v, 0)
            dve_xz(v, 0)
            v.wait_ge(ld_const, LOADED)
            nc.vector.tensor_tensor(gqk[:], col["qn_g"], col["kn_g"], ALU.mult).then_inc(gqk_done, 1)
            nc.vector.tensor_tensor(cen2[:], cenT[:], cenT[:], ALU.mult).then_inc(setup_v, 1)
            nc.vector.tensor_copy(triu[:], triu_f[:]).then_inc(setup_v, 1)
            dve_prep(v, 0, 1)
            dve_prep(v, 0, 3)
            dve_ss(v, 0, 0)
            dve_prep(v, 0, 5)
            dve_stats(v, 1)
            dve_ss(v, 0, 1)
            dve_keys(v, 0)
            dve_prep(v, 0, 7)
            dve_max(v, 0, 0)
            dve_norm1(v, 1)
            dve_stats2(v, 1)
            dve_xz(v, 1)
            v.wait_ge(setup_t, 1)
            nc.vector.tensor_copy(cc[:], X_ps[:, 0:E]).then_inc(x_free, 1)
            dve_body(v, 0, first=True)
            with v.Fori(0, 3) as i:
                dve_body(v, (i, 1, 2))
                dve_body(v, (i, 2, 2))
            dve_body(v, 7, last=True, ahead=False)
            dve_x2(v, 7)
            dve_xf(v, 7)
            dve_top(v, 7)
            dve_place(v, 7)
            dve_weight(v, 7)

            step = [0]

            def chain(ins):
                step[0] += 1
                ins.then_inc(table, 1)
                v.wait_ge(table, step[0])

            def row(x, at, n):
                return tab[:, at:at + n]

            v.wait_ge(counted, 1)
            chain(nc.vector.tensor_copy(counts[:], X_ps[:, 0:E]))
            chain(nc.vector.tensor_tensor(fills[:], counts[:].unsqueeze(2).to_broadcast([P, E, B * S // P]),
                                          tab[:, T_FILL:TAB].unsqueeze(1).to_broadcast([P, E, B * S // P]), ALU.is_gt))
            chain(nc.vector.tensor_reduce(ntiles[:], fills[:], AX.X, ALU.add))
            chain(nc.vector.tensor_tensor(pad_at[:], counts[:], tab[:, T_BASE:T_BASE + E], ALU.add))
            chain(nc.vector.tensor_tensor(cum_terms[:], ntiles[:].unsqueeze(1).to_broadcast([P, E, E]),
                                          tab[:, T_TRI:T_TILE].rearrange("p (e f) -> p e f", e=E), ALU.mult))
            chain(nc.vector.tensor_reduce(cum[:], cum_terms[:], AX.X, ALU.add))
            chain(nc.vector.tensor_tensor(passed, tab[:, T_TILE:T_FILL].unsqueeze(2).to_broadcast([P, TILES, E]),
                                          cum[:].unsqueeze(1).to_broadcast([P, TILES, E]), ALU.is_ge))
            nc.vector.tensor_reduce(expert[:], passed, AX.X, ALU.add)
            chain(nc.vector.tensor_tensor(start_terms, passed, ntiles[:].unsqueeze(1).to_broadcast([P, TILES, E]), ALU.mult))
            chain(nc.vector.tensor_reduce(start[:], start_terms, AX.X, ALU.add))
            nc.vector.tensor_scalar(expert_at[:], expert[:], float(E - 1), None, ALU.min)
            chain(nc.vector.scalar_tensor_tensor(out=since[:], in0=start[:], scalar=-1.0, in1=tab[:, T_TILE:T_FILL],
                                                 op0=ALU.mult, op1=ALU.add))
            chain(nc.vector.tensor_scalar(start[:], since[:], float(P), None, ALU.mult))
            nc.vector.scalar_tensor_tensor(out=row_at[:], in0=expert[:], scalar=float(REGION), in1=start[:],
                                           op0=ALU.mult, op1=ALU.add).then_inc(table, 1)
            assert step[0] + 1 == TABLE_STEPS + 1

            def xT_step(t):
                q = mod(t, 2)
                wait(v, xT_pe, lin(t, 1, 1))
                wait(v, gu_pe, lin(t, 1, 1 - 2))
                nc.vector.tensor_copy(xT_hi[q][:], XT_ps[:, 0:P]).then_inc(xT_hi_set, 1)
                wait(v, xT_hi_set, lin(t, 1, 1))
                nc.vector.tensor_tensor(xT_lo[q][:], XT_ps[:, 0:P], xT_hi[q][:].bitcast(F32), ALU.subtract).then_inc(xT_lo_set, 1)

            def hid_step(t):
                q = mod(t, 2)
                wait(v, gate_set, lin(t, 1, 1))
                wait(v, hT_pe, lin(t, 1, 1 - 2))
                nc.vector.tensor_tensor(hid[q], U_ps[q], gate[q], ALU.mult).then_inc(hid_set, 1)

            def hT_step(t):
                q = mod(t, 2)
                wait(v, hT_hi_set, lin(t, 1, 1))
                nc.vector.tensor_tensor(hT_lo[q][:], HT_ps[0:HP, 0:HC * P], hT_hi[q][:].bitcast(F32), ALU.subtract).then_inc(hT_lo_set, 1)

            xT_step(0)
            tiles(v, lambda t: v_tile(xT_step, hid_step, hT_step, t))
            hT_step(TILES - 1)
            for j in range(4):
                v.wait_ge(y_summed, j + 1)
                if j >= 2:
                    v.wait_ge(stored[j % 2], 16 * (j // 2))
                nc.vector.tensor_tensor(out_sb[j % 2], y_sum[j % 2], x2[:, 4 * j:4 * j + 4, :], ALU.add).then_inc(out_set, 1)

        def act_prep(s, n, step):
            q = par(n)
            wait(s, prep_pe, lin(n, 8, step + 1))
            if step == 0:
                wait(s, prep_pe, lin(n, 8, 4 - 8))
                ins = nc.scalar.activation(lnT[:], M0[:, 0:S], ACT.Identity, bias=col["ln_l_b"], scale=col["ln_l_g"])
            if step == 2:
                wait(s, pv_done, lin(n, UNITS, -UNITS))
                ins = nc.scalar.copy(kvq[q][:, CT, :], M0[:, 0:3 * D])
            if step == 4:
                ins = nc.scalar.copy(kvq[q][:, 0:2, 0:2 * D], M0[:].rearrange("p (t n) -> p t n", t=2))
            if step == 6:
                wait(s, scores_ready, lin(n, UNITS, -UNITS))
                nc.scalar.activation(qT[q][:], M0[:, 0:S], ACT.Copy, scale=gqk[:])
                ins = nc.scalar.copy(kT[q][:, M:NK], M0[:, S:2 * S])
            ins.then_inc(m0_out, 1)

        def act_sq(s, n, part):
            q = par(n)
            wait(s, m0_out, lin(n, 4, part + 2))
            wait(s, m1_out, lin(n, 4, part + 2))
            wait(s, ss_done, lin(n, 2, part - 1))
            if part == 0:
                nc.scalar.activation(sq[:, KT:KT + QT, :], kvq[q][:, CT:KT, 2 * D:3 * D], ACT.Square)
            t0, t1 = ((CT, KT), (0, CT))[part]
            nc.scalar.activation(sq[:, t0:t1, :], kvq[q][:, t0:t1, 0:D], ACT.Square).then_inc(sq_done, 1)

        def act_exp(s, b, u):
            q = u % 2
            wait(s, masked_max, lin(b, UNITS, u + 1))
            wait(s, tb_ready, lin(b, UNITS, u + 1 - 2))
            wait(s, rden_done, lin(b, UNITS, u + 1 - 2))
            nc.scalar.activation(prob[q][:], sm[q][:], ACT.Exp, bias=negmax[:, q:q + 1], scale=-1.0,
                                 accum_out=den[:, q:q + 1]).then_inc(prob_ready, 1)

        def act_pT(s, b, u):
            q = u % 2
            wait(s, ta_ready, lin(b, UNITS, u + 1))
            wait(s, pv_done, lin(b, UNITS, u + 1 - 2))
            nc.scalar.copy(pT[q][:, 0:3 * P], Ta[:, 0:3 * P]).then_inc(pa_ready, 1)
            wait(s, tb_ready, lin(b, UNITS, u + 1))
            nc.scalar.copy(pT[q][:, 3 * P:], Tb[:, 0:3 * P]).then_inc(pb_ready, 1)

        def act_mask(s, b):
            wait(s, masked_max, lin(b, UNITS, -UNITS))
            s.wait_ge(ld_const, LOADED)
            nc.scalar.activation(mbias[par(b)][:, 0:M], mask_u8[:, bass.ds(lin(b, M, 0), M)], ACT.Copy,
                                 bias=-BIG, scale=BIG).then_inc(masked, 1)

        def act_oT(s, m):
            wait(s, post_pe, lin(m, 5, 1))
            nc.scalar.copy(oT[:], X_ps[:, 0:S]).then_inc(oT_ready, 1)

        def act_xf(s, m):
            wait(s, post_pe, lin(m, 5, 3))
            nc.scalar.copy(xfT[:], X_ps[:, 0:S]).then_inc(xfT_ready, 1)
            for t in range(QT):
                ins = nc.scalar.activation(square_scrap[:, t, :], rows_out[par(m)][:, t, 0, 0:D], ACT.Square, accum_out=xx[:, t:t + 1])
            ins.then_inc(xx_done, 1)

        def act_gap(s, m):
            wait(s, dist_done, lin(m, 2, 2))
            nc.scalar.activation(egap[:], dgap[:], ACT.Exp).then_inc(egap_done, 1)

        def act_split(s, e):
            wait(s, w_in, lin(e, 32, 32))
            nc.scalar.copy(w1_hi[:, bass.ds(lin(e, 1, 0), 1), :], w1_in[:].unsqueeze(1))
            nc.scalar.copy(w2_hi[:, bass.ds(lin(e, 1, 0), 1), :], w2_in[:].unsqueeze(1)).then_inc(w_hi, 1)

        def act_body(s, b, first=False, last=False, ahead=True):
            n, m = after(b, 1), after(b, -1)
            act_pT(s, b, 0)
            if not last:
                act_prep(s, n, 0)
            act_exp(s, b, 1)
            if not first:
                act_oT(s, m)
            if not last:
                act_prep(s, n, 2)
            act_pT(s, b, 1)
            if not last:
                act_sq(s, n, 0)
                act_prep(s, n, 4)
            act_exp(s, b, 2)
            if not last:
                act_sq(s, n, 1)
            act_split(s, b)
            act_pT(s, b, 2)
            act_exp(s, b, 3)
            if not first:
                act_xf(s, m)
            if not last:
                act_prep(s, n, 6)
            act_pT(s, b, 3)
            if not last:
                act_exp(s, n, 0)
            if ahead:
                act_mask(s, after(b, 2))
            if not first:
                act_gap(s, m)

        @block.scalar
        def _(s):
            s.wait_ge(ld_const, LOADED)
            s.wait_ge(gqk_done, 1)
            s.wait_ge(zeroed, 2)
            act_mask(s, 0)
            act_mask(s, 1)
            act_prep(s, 0, 0)
            act_prep(s, 0, 2)
            act_sq(s, 0, 0)
            act_prep(s, 0, 4)
            act_sq(s, 0, 1)
            act_prep(s, 0, 6)
            act_exp(s, 0, 0)
            act_body(s, 0, first=True)
            with s.Fori(0, 3) as i:
                act_body(s, (i, 1, 2))
                act_body(s, (i, 2, 2))
            act_body(s, 7, last=True, ahead=False)
            act_oT(s, 7)
            act_xf(s, 7)
            act_gap(s, 7)

            def gate_step(t):
                q = mod(t, 2)
                wait(s, gu_pe, lin(t, 1, 1))
                wait(s, hid_set, lin(t, 1, 1 - 2))
                nc.scalar.activation(gate[q], G_ps[q], ACT.Silu).then_inc(gate_set, 1)

            def hT_step(t):
                q = mod(t, 2)
                wait(s, hT_pe, lin(t, 1, 1))
                wait(s, y_pe, lin(t, 1, 1 - 2))
                nc.scalar.copy(hT_hi[q][:], HT_ps[0:HP, 0:HC * P]).then_inc(hT_hi_set, 1)

            def y_step(t):
                q = mod(t, RING)
                wait(s, y_pe, lin(t, 1, 1))
                wait(s, y_out[q], part_of(t, RING, 16, 0))
                nc.scalar.activation(y[q], Y_ps[:, 0:D], ACT.Copy, scale=xt[q][:, D:D + 1]).then_inc(y_set, 1)

            def tile(t):
                if t != 0:
                    hT_step(after(t, -1))
                gate_step(t)
                if t not in (0, 1):
                    y_step(after(t, -2))

            tiles(s, tile)
            hT_step(TILES - 1)
            y_step(TILES - 2)
            y_step(TILES - 1)

        def pe_prep(t_, n, step):
            q = par(n)
            bank_ = (M0, M1)[step % 2]
            wait(t_, (m0_out, m1_out)[step % 2], lin(n, 4, step // 2))
            if step == 0:
                wait(t_, xz_done, lin(n, 1, 1))
                for t in range(QT):
                    ins = nc.tensor.transpose(bank_[:, t * P:(t + 1) * P], xz[:, q, t, :], eye[:])
            if step == 1:
                wait(t_, norm1_done, lin(n, 2, 2))
                for t in range(CT):
                    ins = nc.tensor.transpose(bank_[0:C, t * P:(t + 1) * P], cn[:, q, t, :], eye[:])
            if step in (2, 3):
                if step == 2:
                    wait(t_, m0_out, lin(n, 4, 1))
                t = step - 2
                ins = nc.tensor.matmul(bank_[:, 0:3 * D], lnT[:, t * P:(t + 1) * P], wqkv_l[:], start=True, stop=True)
            if step in (4, 5):
                if step == 4:
                    wait(t_, m1_out, lin(n, 4, 1))
                for j in range(2):
                    t = 2 * (step - 4) + j
                    ins = nc.tensor.matmul(bank_[:, j * 2 * D:(j + 1) * 2 * D], cT[:, t * P:(t + 1) * P], wkv_c[:],
                                           start=True, stop=True)
            if step == 6:
                wait(t_, knl_done, lin(n, 1, 1))
                for t in range(QT):
                    nc.tensor.transpose(bank_[:, t * P:(t + 1) * P], kvq[q][:, CT + t, 2 * D:3 * D], eye[:])
                for t in range(QT):
                    ins = nc.tensor.transpose(bank_[:, S + t * P:S + (t + 1) * P], kn[:, CT + t, :], eye[:])
            if step == 7:
                wait(t_, knc_done, lin(n, 1, 1))
                for t in range(CT):
                    ins = nc.tensor.transpose(bank_[:, t * P:(t + 1) * P], kn[:, t, :], eye[:])
            ins.then_inc(prep_pe, 1)

        def pe_scores(t_, b, u):
            q, (t, h) = par(b), divmod(u, H)
            if u == 0:
                wait(t_, m0_out, lin(b, 4, 4))
                wait(t_, m1_out, lin(b, 4, 4))
            wait(t_, masked_max, lin(b, UNITS, u))
            r = slice(h * DH, (h + 1) * DH)
            nc.tensor.matmul(S_ps[:, 0:M], qT[q][r, t * P:(t + 1) * P], kT[q][r, 0:M], start=True, stop=True)
            nc.tensor.matmul(S_ps[:, M:NK], qT[q][r, t * P:(t + 1) * P], kT[q][r, M:NK], start=True,
                             stop=True).then_inc(scores_ready, 1)

        def pe_pT(t_, b, u):
            q = u % 2
            wait(t_, prob_ready, lin(b, UNITS, u + 1))
            wait(t_, pa_ready, lin(b, UNITS, u))
            for j in range(3):
                ins = nc.tensor.transpose(Ta[:, j * P:(j + 1) * P], prob[q][:, j * P:(j + 1) * P], eye[:])
            ins.then_inc(ta_ready, 1)
            wait(t_, pb_ready, lin(b, UNITS, u))
            for j in range(3):
                ins = nc.tensor.transpose(Tb[:, j * P:(j + 1) * P], prob[q][:, (3 + j) * P:(4 + j) * P], eye[:])
            ins.then_inc(tb_ready, 1)

        def pe_pv(t_, b, u):
            q, (t, h) = u % 2, divmod(u, H)
            wait(t_, pa_ready, lin(b, UNITS, u + 1))
            wait(t_, pb_ready, lin(b, UNITS, u + 1))
            wait(t_, o_ready, lin(b, UNITS, u))
            for j in range(KT):
                ins = nc.tensor.matmul(O_ps[:, 0:DH], pT[q][:, j * P:(j + 1) * P],
                                       kvq[par(b)][:, j, D + h * DH:D + (h + 1) * DH], start=(j == 0), stop=(j == KT - 1))
            ins.then_inc(pv_done, 1)

        def pe_post(t_, m, step):
            if step == 0:
                wait(t_, o_ready, lin(m, UNITS, UNITS))
                wait(t_, x_free, lin(m, 1, 1))
                for t in range(QT):
                    ins = nc.tensor.transpose(X_ps[:, t * P:(t + 1) * P], o_sb[:, t, :], eye[:])
            if step == 1:
                wait(t_, oT_ready, lin(m, 1, 1))
                for t in range(QT):
                    ins = nc.tensor.matmul(X_ps[:, t * D:(t + 1) * D], oT[:, t * P:(t + 1) * P], wo[:], start=True, stop=True)
            if step == 2:
                wait(t_, xf_done, lin(m, 1, 1))
                for t in range(QT):
                    ins = nc.tensor.transpose(X_ps[:, t * P:(t + 1) * P], rows_out[par(m)][:, t, 0, 0:D], eye[:])
            if step == 3:
                wait(t_, xfT_ready, lin(m, 1, 1))
                for t in range(QT):
                    ins = nc.tensor.matmul(X_ps[:, t * E:(t + 1) * E], xfT[:, t * P:(t + 1) * P], cenT[:], start=True, stop=True)
            if step == 4:
                wait(t_, router_done, lin(m, 6, 6))
                nc.tensor.matmul(X_ps[:, 0:E], triu[:], picks[:, 0, :], start=True, stop=False)
                nc.tensor.matmul(X_ps[:, 0:E], ones[:], before_b[:], start=False, stop=True)
                nc.tensor.matmul(X_ps[:, E:2 * E], triu[:], picks[:, 1, :], start=True, stop=False)
                nc.tensor.matmul(X_ps[:, E:2 * E], ones[:], picks[:, 0, :], start=False, stop=False)
                ins = nc.tensor.matmul(X_ps[:, E:2 * E], ones[:], before_b[:], start=False, stop=True)
            ins.then_inc(post_pe, 1)

        def pe_body(t_, b, first=False, last=False):
            n, m = after(b, 1), after(b, -1)
            pe_pT(t_, b, 0)
            if not last:
                pe_prep(t_, n, 0)
            pe_scores(t_, b, 1)
            if not last:
                pe_prep(t_, n, 1)
            if not first:
                pe_post(t_, m, 0)
            pe_pv(t_, b, 0)
            if not last:
                pe_prep(t_, n, 2)
                pe_prep(t_, n, 3)
            pe_pT(t_, b, 1)
            if not first:
                pe_post(t_, m, 1)
            if not last:
                pe_prep(t_, n, 4)
            pe_scores(t_, b, 2)
            if not last:
                pe_prep(t_, n, 5)
            pe_pv(t_, b, 1)
            pe_pT(t_, b, 2)
            pe_scores(t_, b, 3)
            pe_pv(t_, b, 2)
            if not first:
                pe_post(t_, m, 2)
            if not last:
                pe_prep(t_, n, 6)
            pe_pT(t_, b, 3)
            if not first:
                pe_post(t_, m, 3)
            if not last:
                pe_prep(t_, n, 7)
                pe_scores(t_, n, 0)
            pe_pv(t_, b, 3)
            if not first:
                pe_post(t_, m, 4)

        @block.tensor
        def _(t_):
            t_.wait_ge(ld_const, LOADED)
            for step in range(8):
                pe_prep(t_, 0, step)
            pe_scores(t_, 0, 0)
            t_.wait_ge(setup_v, 2)
            nc.tensor.matmul(X_ps[:, 0:E], ones_f[:], cen2[:], start=True, stop=True).then_inc(setup_t, 1)
            pe_body(t_, 0, first=True)
            with t_.Fori(0, 3) as i:
                pe_body(t_, (i, 1, 2))
                pe_body(t_, (i, 2, 2))
            pe_body(t_, 7, last=True)
            for step in range(5):
                pe_post(t_, 7, step)
            t_.wait_ge(before_done, 3 * B)
            nc.tensor.matmul(X_ps[:, 0:E], ones[:], before_b[:], start=True, stop=True).then_inc(counted, 1)

            def expert_of(t):
                return t_.value_load(expert_at[0:1, bass.ds(lin(t, 1, 0), 1)], min_val=0, max_val=E - 1)

            def xT_step(t):
                wait(t_, xt_in[mod(t, RING)], part_of(t, RING, 16, 16))
                wait(t_, xT_lo_set, lin(t, 1, 0))
                nc.tensor.transpose(XT_ps[:, 0:P], xt[mod(t, RING)][:, 0:D], eye[:]).then_inc(xT_pe, 1)

            def gu_step(t, e):
                q = mod(t, 2)
                wait(t_, xT_lo_set, lin(t, 1, 1))
                wait(t_, hid_set, lin(t, 1, 1 - 2))
                for o, at in ((G_ps[q], 0), (U_ps[q], HID)):
                    nc.tensor.matmul(o, ones[0:3, :], bias[:, bass.ds(e, 1), at:at + HID].rearrange("p o n -> p (o n)"),
                                     start=True, stop=False)
                    for n, (x_, w_) in enumerate(((xT_hi, w1_hi), (xT_hi, w1_lo), (xT_lo, w1_hi))):
                        ins = nc.tensor.matmul(o, x_[q][:], w_[:, bass.ds(e, 1), at:at + HID].rearrange("p o n -> p (o n)"),
                                               start=False, stop=(n == 2))
                ins.then_inc(gu_pe, 1)

            def hT_step(t):
                q = mod(t, 2)
                wait(t_, hid_set, lin(t, 1, 1))
                wait(t_, hT_lo_set, lin(t, 1, 0))
                for c in range(HC):
                    ins = nc.tensor.transpose(HT_ps[0:HP, c * P:(c + 1) * P], hid[q][:, c * HP:(c + 1) * HP], eye[:])
                ins.then_inc(hT_pe, 1)

            def y_step(t, e):
                q = mod(t, 2)
                wait(t_, hT_lo_set, lin(t, 1, 1))
                wait(t_, y_set, lin(t, 1, 1))
                nc.tensor.matmul(Y_ps[:, 0:D], ones[0:3, :], bias[:, bass.ds(e, 1), 2 * HID:].rearrange("p o n -> p (o n)"),
                                 start=True, stop=False)
                for c in range(HC):
                    for n, (h_, w_) in enumerate(((hT_hi, w2_hi), (hT_hi, w2_lo), (hT_lo, w2_hi))):
                        ins = nc.tensor.matmul(Y_ps[:, 0:D], h_[q][:, c * P:(c + 1) * P],
                                               w_[:, bass.ds(e, 1), c * D:(c + 1) * D].rearrange("p o n -> p (o n)"),
                                               start=False, stop=(c == HC - 1 and n == 2))
                ins.then_inc(y_pe, 1)

            t_.wait_ge(table, TABLE_STEPS + 1)
            t_.wait_ge(w_lo, E)
            t_.wait_ge(bias_set, 16 * 3)
            xT_step(0)

            at_hand = []

            def tile(t):
                if not isinstance(t, int) and t[1] == FIRST:
                    at_hand[:] = [expert_of(after(t, -2)), expert_of(after(t, -1))]
                if t == TILES - 1:
                    at_hand[:] = [expert_of(t - 2), expert_of(t - 1)]
                if t != TILES - 1:
                    xT_step(after(t, 1))
                if t != 0:
                    hT_step(after(t, -1))
                at_hand.append(expert_of(t))
                gu_step(t, at_hand[-1])
                if t not in (0, 1):
                    y_step(after(t, -2), at_hand.pop(0))

            tiles(t_, tile)
            hT_step(TILES - 1)
            y_step(TILES - 2, at_hand[0])
            y_step(TILES - 1, at_hand[1])


def kernel(**inputs):
    import concourse.bacc as bacc
    from concourse.bass_utils import run_bass_kernel_spmd

    g = {k: np.asarray(v) for k, v in inputs.items()}
    xa = {k[len("L0_xattn_"):]: v for k, v in g.items() if k.startswith("L0_xattn_")}
    fa = {k[len("L0_ffn_"):]: v for k, v in g.items() if k.startswith("L0_ffn_")}
    two = lambda v: np.concatenate([v, v])
    wide = lambda v: np.concatenate([v, np.zeros(P - v.shape[0], v.dtype)])
    arrays = {
        "x": g["x"].reshape(B * S, D),
        "ctx": g["ctx_768"].reshape(B * M, C),
        "mask": g["mask_BxS2_bk0"],
        "wqkv_l": np.concatenate([xa["Wlkv"], xa["Wq"]]).T,
        "wkv_c": xa["Wkv"].T,
        "wo": xa["Wo"].T,
        "bo": xa["bo"],
        "cols": np.stack([wide(xa["ln_x_g"]), wide(xa["ln_x_b"]), xa["ln_l_g"], xa["ln_l_b"],
                          two(xa["qn_g"]), two(xa["kn_g"])], axis=1),
        "tab": np.broadcast_to(np.concatenate([
            np.arange(E), REGION * np.arange(E), np.tri(E).reshape(-1), np.arange(TILES),
            P * np.arange(B * S // P)]).astype(np.float32), (P, TAB)),
        "slot_tab": (TOP * (P * np.arange(B * QT)[None, :, None] + np.arange(P)[:, None, None])
                     + np.arange(TOP)[None, None, :]).astype(np.int32),
        "triu": np.triu(np.ones((P, P), np.float32), 1),
        "cenT": fa["centroid"].T,
        "w1": np.concatenate([fa["Wg"], fa["W1"]], axis=2).transpose(1, 0, 2).reshape(D, E * 2 * HID),
        "w2": fa["W2"].reshape(E, HC, HP, D).transpose(2, 0, 1, 3).reshape(HP, E * HC * D),
        "bias": np.concatenate([fa["bg"], fa["b1"], fa["b2"]], axis=1),
        "eye": np.eye(P, dtype=np.float32),
    }
    arrays = {k: np.ascontiguousarray(v) for k, v in arrays.items()}
    nc = bacc.Bacc("TRN2", target_bir_lowering=False, num_devices=1)
    dram = {k: nc.dram_tensor(f"in_{k}", v.shape, mybir.dt.from_np(v.dtype), kind="ExternalInput").ap()
            for k, v in arrays.items()}
    out = nc.dram_tensor("out_0", (B * S, D), F32, kind="ExternalOutput").ap()
    build(nc, dram, out)
    r = run_bass_kernel_spmd(nc, [{f"in_{k}": v for k, v in arrays.items()}], core_ids=[0])
    return r.results[0]["out_0"].reshape(B, S, D)
```

```python
from contextlib import ExitStack

import numpy as np

import concourse.bass as bass
from concourse import mybir

ALU = mybir.AluOpType
ACT = mybir.ActivationFunctionType
AX = mybir.AxisListType
F32 = mybir.dt.float32
F32R = mybir.dt.float32r
BF16 = mybir.dt.bfloat16
U8 = mybir.dt.uint8
I32 = mybir.dt.int32
U32 = mybir.dt.uint32

P = 128
B, S, D = 8, 256, 128
M, C = 512, 96
H, DH = 2, 64
QT, CT = S // P, M // P
KT = CT + QT
NK = KT * P
UNITS = QT * H
E, HID, HC = 8, 342, 3
HP = HID // HC
TOP = 2
ROW = D + 2
REGION = P + B * S
RING = 8
TILES = B * S * TOP // P + E - 1
FIRST = RING + (TILES - 1) % RING
GROUPS = (TILES - 1) // RING
SPARE = E
NOWHERE = 1 << 20
LN_EPS = 1e-5
RMS_FLOOR = 1e-16
BIG = 1e30
T_IOTA, T_BASE, T_TRI, T_TILE, T_ROWS, T_FILL, T_POW, TAB = np.cumsum(
    [0, E, E + 1, (E + 1) * E, TILES, TILES, B * S // P, RING]).tolist()
COLS = ["ln_x_g", "ln_x_b", "ln_l_g", "ln_l_b", "qn_g", "kn_g"]


def lin(b, per, k):
    if isinstance(b, int):
        return per * b + k
    i, c, n = b
    return i * (n * per) + (per * c + k)


def after(b, d):
    return b + d if isinstance(b, int) else (b[0], b[1] + d, b[2])


def mod(b, m):
    return b % m if isinstance(b, int) else b[1] % m


def part_of(b, m, per, k):
    if isinstance(b, int):
        return per * (b // m) + k
    i, c, n = b
    return i * (n // m * per) + (per * (c // m) + k)


def par(b):
    return mod(b, 2)


def wait(eng, sem, value):
    if isinstance(value, int) and value <= 0:
        return
    eng.wait_ge(sem, value)


def build(nc, a, out):
    with ExitStack() as ctx:
        def sb(name, shape, dt=F32):
            return ctx.enter_context(nc.sbuf_tensor(name, shape, dt))

        def bank(name, shape):
            return ctx.enter_context(nc.psum_tensor(name, shape, F32))

        def sem(name):
            return ctx.enter_context(nc.semaphore(name))

        xs = [sb(f"xs{p}", [P, QT, D]) for p in range(2)]
        cs = [sb(f"cs{p}", [P, CT, C]) for p in range(2)]
        xb = sb("xb", [P, (B + 1) * QT, D])
        mask_u8 = sb("mask_u8", [P, (B + 1) * M], U8)
        mbias = [sb(f"mbias{p}", [P, NK]) for p in range(2)]
        wqkv_l = sb("wqkv_l", [P, 3 * D])
        wkv_c = sb("wkv_c", [C, 2 * D])
        wo = sb("wo", [P, D])
        cols = sb("cols", [P, len(COLS)])
        gqk = sb("gqk", [P, 1])
        bo_b = sb("bo_b", [P, D])
        eye = sb("eye", [P, P])
        neghalf = sb("neghalf", [P, 16])
        stat = sb("stat", [P, CT + QT, 6])
        mv = sb("mv", [P, CT + QT, 2])
        stat2 = sb("stat2", [P, QT, 6])
        mv2 = sb("mv2", [P, QT, 2])
        var = sb("var", [P, CT + QT])
        rstd = sb("rstd", [P, CT + QT])
        var2 = sb("var2", [P, QT])
        rstd2 = sb("rstd2", [P, QT])
        xhat = sb("xhat", [P, QT, D])
        xz = sb("xz", [P, 2, QT, D])
        cn = sb("cn", [P, 2, CT, C])
        lnT = sb("lnT", [P, S])
        cT = sb("cT", [C, M])
        kvq = [sb(f"kvq{p}", [P, KT, 3 * D]) for p in range(2)]
        sq = sb("sq", [P, KT + QT, D])
        ss = sb("ss", [P, (KT + QT) * H])
        ssf = sb("ssf", [P, (KT + QT) * H])
        rms = sb("rms", [P, (KT + QT) * H])
        nrq = sb("nrq", [P, 2, QT * H])
        kn = sb("kn", [P, KT, D])
        qT = [sb(f"qT{p}", [P, S]) for p in range(2)]
        kT = [sb(f"kT{p}", [P, NK]) for p in range(2)]
        sm = [sb(f"sm{p}", [P, NK]) for p in range(2)]
        negmax = sb("negmax", [P, 2])
        prob = [sb(f"prob{p}", [P, NK]) for p in range(2)]
        den = sb("den", [P, 2])
        rden = sb("rden", [P, 2])
        pT = [sb(f"pT{p}", [P, NK]) for p in range(2)]
        o_sb = sb("o_sb", [P, QT, D])
        oT = sb("oT", [P, S])
        x2 = xb
        stat3 = sb("stat3", [P, QT, 6])
        mv3 = sb("mv3", [P, QT, 2])
        var3 = sb("var3", [P, QT])
        rstd3 = sb("rstd3", [P, QT])
        rows_out = [sb(f"rows_out{p}", [P, QT, TOP, ROW]) for p in range(2)]
        xfT = sb("xfT", [P, S])
        square_scrap = sb("square_scrap", [P, QT, D], BF16)
        xx = sb("xx", [P, QT])
        cenT = sb("cenT", [P, E])
        cen2 = sb("cen2", [P, E])
        cc = sb("cc", [P, E])
        d2raw = sb("d2raw", [P, QT, E])
        d2 = sb("d2", [P, QT, E])
        best = sb("best", [P, QT, 8])
        choice = sb("choice", [P, QT, 8], U32)
        dist = sb("dist", [P, QT, TOP])
        dgap = sb("dgap", [P, QT])
        egap = sb("egap", [P, QT])
        esum = sb("esum", [P, QT])
        onehot = sb("onehot", [P, QT, TOP, E])
        picks = sb("picks", [P, QT, E], BF16)
        before = sb("before", [P, E])
        before_b = sb("before_b", [P, E], BF16)
        before_t = sb("before_t", [P, E])
        ranks = sb("ranks", [P, QT, E])
        ranked = sb("ranked", [P, QT, TOP, E])
        pos_f = sb("pos_f", [P, QT * TOP])
        pos = [sb(f"pos{p}", [P, QT * TOP], U32) for p in range(2)]
        tab = sb("tab", [P, TAB])
        slot_tab = sb("slot_tab", [P, (B + 1) * QT, TOP], I32)
        triu_f = sb("triu_f", [P, P])
        triu = sb("triu", [P, P], BF16)
        ones_f = sb("ones_f", [P, P])
        ones = sb("ones", [P, P], BF16)
        half_ = sb("half_", [P, QT * TOP])
        pad_row = sb("pad_row", [P, ROW])
        counts = sb("counts", [P, E])
        fills = sb("fills", [P, E, B * S // P])
        ntiles = sb("ntiles", [P, E])
        cum_terms = sb("cum_terms", [P, E + 1, E])
        cum = sb("cum", [P, E + 1])
        ends = sb("ends", [P, E + 1])
        offset = sb("offset", [P, E + 1])
        jump = sb("jump", [P, E])
        passed = sm[0][:, 0:TILES * E].rearrange("p (t e) -> p t e", e=E)
        expert = sb("expert", [P, TILES])
        start_terms = sm[1][:, 0:TILES * E].rearrange("p (t e) -> p t e", e=E)
        start = sb("start", [P, TILES])
        row_at = sb("row_at", [P, TILES], I32)
        expert_at = sb("expert_at", [P, TILES], I32)
        digits = sb("digits", [P, GROUPS, RING])
        grouped = sb("grouped", [P, GROUPS])
        group_at = sb("group_at", [P, GROUPS], I32)
        w1_in = sb("w1_in", [P, 2 * HID])
        w2_in = sb("w2_in", [HP, HC * D])
        w1_hi = sb("w1_hi", [P, E, 2 * HID], F32R)
        w1_lo = sb("w1_lo", [P, E, 2 * HID], F32R)
        w2_parts = sb("w2_parts", [HP, E, HC, 2, D], F32R)
        BW = 2 * HID + D
        BP = next(p for p in range(P, 0, -1) if E * BW % p == 0)
        bias_in = sb("bias_in", [BP, E * BW // BP])
        bias_rest = sb("bias_rest", [BP, E * BW // BP])
        bias_part = [sb(f"bias_part{i}", [BP, E * BW // BP], BF16) for i in range(3)]
        bias = sb("bias", [3, E, BW], BF16)
        xT_hi = [sb(f"xT_hi{i}", [P, P], F32R) for i in range(2)]
        xT_lo = [sb(f"xT_lo{i}", [P, P], F32R) for i in range(2)]
        gate = [pT[i][:, 0:HID] for i in range(2)]
        hid = [prob[i][:, 0:HID] for i in range(2)]
        hT_hi = [sb(f"hT_hi{i}", [HP, HC * P], F32R) for i in range(2)]
        hT_lo = [sb(f"hT_lo{i}", [HP, HC * P], F32R) for i in range(2)]
        done = [kvq[i][:].rearrange("p t n -> p (t n)") for i in range(2)]
        xt = [done[0][:, i * ROW:(i + 1) * ROW] for i in range(RING)]
        y = [done[1][:, i * D:(i + 1) * D] for i in range(RING)]
        y_in = [done[i // 2][:, i % 2 * 8 * D:(i % 2 + 1) * 8 * D].rearrange("p (t k d) -> p t k d", k=TOP, d=D)
                for i in range(4)]
        out_sb = [t[:, 0:4 * D].rearrange("p (t d) -> p t d", d=D) for t in (sm[0], sm[1], prob[0], prob[1])]

        S_ps = bank("S_ps", [P, 1024])
        Ta = bank("Ta", [P, 512])
        Tb = bank("Tb", [P, 512])
        O_ps = bank("O_ps", [P, 512])
        M0 = bank("M0", [P, 512])
        M1 = bank("M1", [P, 512])
        X_ps = bank("X_ps", [P, 512])

        G_ps = [S_ps[:, 0:HID], S_ps[:, 512:512 + HID]]
        U_ps = [Ta[:, 0:HID], Tb[:, 0:HID]]
        HT_ps = [M0, X_ps]
        Y_ps, XT_ps = O_ps[:, 0:2 * D], M1[:, 0:P]

        sorted_rows = nc.dram_tensor("sorted_rows", (E * REGION + SPARE * P, ROW), F32).ap()
        results = nc.dram_tensor("results", (B * S * TOP, D), F32).ap()

        ld_const = sem("ld_const")
        rows_in = [sem(f"rows_in{p}") for p in range(2)]
        zeroed = sem("zeroed")
        masked = sem("masked")
        gqk_done = sem("gqk_done")
        stat1_done = sem("stat1_done")
        rstd1_done = sem("rstd1_done")
        norm1_done = sem("norm1_done")
        stat2_done = sem("stat2_done")
        rstd2_done = sem("rstd2_done")
        xz_done = sem("xz_done")
        xb_done = sem("xb_done")
        prep_pe = sem("prep_pe")
        m0_out = sem("m0_out")
        m1_out = sem("m1_out")
        sq_done = sem("sq_done")
        ss_done = sem("ss_done")
        floor_done = sem("floor_done")
        rms_done = sem("rms_done")
        nrq_done = sem("nrq_done")
        knl_done = sem("knl_done")
        knc_done = sem("knc_done")
        scores_ready = sem("scores_ready")
        masked_max = sem("masked_max")
        prob_ready = sem("prob_ready")
        ta_ready = sem("ta_ready")
        tb_ready = sem("tb_ready")
        pa_ready = sem("pa_ready")
        pb_ready = sem("pb_ready")
        pv_done = sem("pv_done")
        rden_done = sem("rden_done")
        o_ready = sem("o_ready")
        post_pe = sem("post_pe")
        oT_ready = sem("oT_ready")
        x2_ready = sem("x2_ready")
        stat3_done = sem("stat3_done")
        rstd3_done = sem("rstd3_done")
        xf_done = sem("xf_done")
        xfT_ready = sem("xfT_ready")
        xx_done = sem("xx_done")
        router_done = sem("router_done")
        dist_done = sem("dist_done")
        egap_done = sem("egap_done")
        weight_done = sem("weight_done")
        slot_done = sem("slot_done")
        x_free = sem("x_free")
        pos_done = sem("pos_done")
        before_done = sem("before_done")
        scattered = [sem(f"scattered{p}") for p in range(2)]
        w_in = sem("w_in")
        w_hi = sem("w_hi")
        w_lo = sem("w_lo")
        bias_ld = sem("bias_ld")
        bias_chain = sem("bias_chain")
        bias_set = sem("bias_set")
        setup_v = sem("setup_v")
        setup_t = sem("setup_t")
        counted = sem("counted")
        table = sem("table")
        xt_in = [sem(f"xt_in{i}") for i in range(RING)]
        y_out = [sem(f"y_out{i}") for i in range(RING)]
        xT_pe = sem("xT_pe")
        xT_hi_set = sem("xT_hi_set")
        xT_lo_set = sem("xT_lo_set")
        gu_pe = sem("gu_pe")
        gate_set = sem("gate_set")
        hid_set = sem("hid_set")
        hT_pe = sem("hT_pe")
        hT_hi_set = sem("hT_hi_set")
        hT_lo_set = sem("hT_lo_set")
        y_pe = sem("y_pe")
        y_half = sem("y_half")
        y_set = sem("y_set")
        y_back = [sem(f"y_back{i}") for i in range(4)]
        out_set = [sem(f"out_set{i}") for i in range(4)]
        stored = sem("stored")

        col = {n: cols[:, i:i + 1] for i, n in enumerate(COLS)}
        x_v = a["x"].rearrange("(t p) d -> p t d", p=P)
        c_v = a["ctx"].rearrange("(t p) d -> p t d", p=P)
        out_v = out.rearrange("(t p) d -> p t d", p=P)
        w1_v = a["w1"].rearrange("p (e n) -> p e n", e=E)
        w2_v = a["w2"].rearrange("p (e n) -> p e n", e=E)
        res_v = results.rearrange("(t p k) d -> p t k d", p=P, k=TOP)
        TABLE_STEPS = 13
        LOADED = 16 * 11

        block = ctx.enter_context(nc.Block())

        def add_results(eng, compute, j):
            eng.wait_ge(y_back[j], 16)
            compute.tensor_tensor(out_sb[j], y_in[j][:, :, 0, :], y_in[j][:, :, 1, :], ALU.add).then_inc(out_set[j], 1)
            eng.wait_ge(out_set[j], 1)
            compute.tensor_tensor(out_sb[j], out_sb[j], x2[:, 4 * j:4 * j + 4, :], ALU.add).then_inc(out_set[j], 1)

        def held(eng, *waits):
            values = [v if isinstance(v, int) else eng.to_reg(v) for _, v in waits]
            eng.wait_ge(zeroed, 1)
            for (s, _), v in zip(waits, values):
                wait(eng, s, v)

        def load_rows(sp, n):
            q = par(n)
            if not isinstance(n, int):
                held(sp, (norm1_done, lin(n, 2, 2 - 4)),
                         (xb_done, lin(n, 1, 1 - 2)))
            sp.dma_start(xs[q][:], x_v[:, bass.ds(lin(n, QT, 0), QT), :]).then_inc(rows_in[q], 16)
            sp.dma_start(cs[q][:], c_v[:, bass.ds(lin(n, CT, 0), CT), :]).then_inc(rows_in[q], 16)

        def load_weights(sp, e):
            held(sp, (w_hi, lin(e, 1, 0)),
                     (w_lo, lin(e, 1, 0)))
            sp.dma_start(w1_in[:], w1_v[:, bass.ds(lin(e, 1, 0), 1), :]).then_inc(w_in, 16)
            sp.dma_start(w2_in[:], w2_v[:, bass.ds(lin(e, 1, 0), 1), :]).then_inc(w_in, 16)

        def tiles(eng, step):
            for t in range(FIRST):
                step(t)
            with eng.Fori(0, (TILES - 1 - FIRST) // RING) as i:
                for c in range(RING):
                    step((i, FIRST + c, RING))
            step(TILES - 1)

        @block.sync
        def _(sp):
            load_rows(sp, 0)
            for t, n in ((cols, "cols"), (eye, "eye"), (wqkv_l, "wqkv_l"), (wkv_c, "wkv_c")):
                sp.dma_start(t[:], a[n]).then_inc(ld_const, 16)
            sp.dma_start(mask_u8[:, 0:B * M], a["mask"].rearrange("b m -> (b m)").partition_broadcast(P)).then_inc(ld_const, 16)
            sp.dma_start(wo[:], a["wo"]).then_inc(ld_const, 16)
            sp.dma_start(bo_b[:], a["bo"].partition_broadcast(P)).then_inc(ld_const, 16)
            sp.dma_start(tab[:], a["tab"]).then_inc(ld_const, 16)
            sp.dma_start(slot_tab[:, 0:B * QT, :], a["slot_tab"]).then_inc(ld_const, 16)
            sp.dma_start(triu_f[:], a["triu"]).then_inc(ld_const, 16)
            sp.dma_start(cenT[:], a["cenT"]).then_inc(ld_const, 16)
            load_rows(sp, 1)
            load_weights(sp, 0)
            sp.dma_start(bias_in[:], a["bias"].rearrange("(p n) -> p n", p=BP)).then_inc(bias_ld, 16)
            with sp.Fori(0, 3) as i:
                for c in (2, 3):
                    load_rows(sp, (i, c, 2))
                    load_weights(sp, (i, c - 1, 2))
            sp.wait_ge(rows_in[0], 32 * B // 2)
            sp.sem_inc(rows_in[0], 32)
            load_weights(sp, E - 1)
            sp.wait_ge(bias_chain, 5)
            for j in range(3):
                sp.dma_start(bias[j:j + 1, :, :], bias_part[j][:]).then_inc(bias_set, 16)
            sp.wait_ge(table, TABLE_STEPS)
            for q in range(2):
                sp.wait_ge(scattered[q], 64 + 64 * B // 2)

            def load_tile(t):
                q = mod(t, RING)
                held(sp, (y_out[q], part_of(t, RING, 16, 0)))
                row = sp.value_load(row_at[0:1, bass.ds(lin(t, 1, 0), 1)], min_val=0, max_val=(E * REGION + SPARE * P) - P)
                sp.dma_start(xt[q], sorted_rows[bass.ds(row, P), :]).then_inc(xt_in[q], 16)

            tiles(sp, load_tile)
            for q in range(RING):
                sp.wait_ge(y_out[q], 16 * len(range(q, TILES, RING)))
            for j in range(4):
                sp.dma_start(y_in[j], res_v[:, 4 * j:4 * j + 4, :, :]).then_inc(y_back[j], 16)
            for j in range(4):
                sp.wait_ge(out_set[j], 2)
                sp.dma_start(out_v[:, 4 * j:4 * j + 4, :], out_sb[j]).then_inc(stored, 16)
            sp.wait_ge(stored, 16 * 4)

        def pool_pow(p, out_, in_, power):
            return nc.gpsimd.tensor_tensor(out_, in_, power, ALU.pow)

        def pool_rstd(p, n, var_, rstd_, mean_var, stats, own):
            held(p, (stats, lin(n, 2, 2)))
            nc.gpsimd.tensor_scalar(var_, mean_var[:, :, 1], LN_EPS, None, ALU.add).then_inc(own, 1)
            wait(p, own, lin(n, 2, 1))
            w = mean_var.shape[1]
            nc.gpsimd.tensor_tensor(rstd_, var_, neghalf[:, 0:w], ALU.pow).then_inc(own, 1)

        def pool_rstd1(p, n):
            pool_rstd(p, n, var[:], rstd[:], mv, stat1_done, rstd1_done)

        def pool_rstd2(p, n):
            pool_rstd(p, n, var2[:], rstd2[:], mv2, stat2_done, rstd2_done)

        def pool_rstd3(p, m):
            pool_rstd(p, m, var3[:], rstd3[:], mv3, stat3_done, rstd3_done)

        def pool_xb(p, n):
            q = par(n)
            held(p, (rows_in[q], part_of(n, 2, 32, 32)))
            nc.gpsimd.tensor_tensor(xb[:, bass.ds(lin(n, QT, 0), QT), :], xs[q][:],
                                    bo_b[:].unsqueeze(1).to_broadcast([P, QT, D]), ALU.add).then_inc(xb_done, 1)

        def pool_router(p, m):
            q = par(m)
            held(p, (scattered[q], part_of(m, 2, 64, 64)))
            nc.gpsimd.tensor_copy(rows_out[q][:].bitcast(I32)[:, :, :, D + 1],
                                  slot_tab[:, bass.ds(lin(m, QT, 0), QT), :]).then_inc(slot_done, 1)
            wait(p, router_done, lin(m, 6, 3))
            nc.gpsimd.tensor_tensor(dist[:], best[:, :, 0:TOP], half_[:].rearrange("p (t k) -> p t k", k=TOP),
                                    ALU.pow).then_inc(dist_done, 1)
            wait(p, dist_done, lin(m, 2, 1))
            nc.gpsimd.tensor_tensor(dgap[:], dist[:, :, 1], dist[:, :, 0], ALU.subtract).then_inc(dist_done, 1)

        def pool_scatter(p, m):
            q = par(m)
            held(p, (pos_done, lin(m, 3, 3)),
                    (weight_done, lin(m, 3, 3)),
                    (slot_done, lin(m, 1, 1)))
            for t in range(QT):
                for k in range(TOP):
                    nc.gpsimd.indirect_dma_start(
                        out=sorted_rows[:, :],
                        out_offset=bass.IndirectOffsetOnAxis(ap=pos[q][:, TOP * t + k:TOP * t + k + 1], axis=0),
                        in_=rows_out[q][:, t, k, :], in_offset=None).then_inc(scattered[q], 16)

        def pool_rms(p, n, part):
            q = par(n)
            c0, c1 = ((CT * H, (KT + QT) * H), (0, CT * H))[part]
            held(p, (ss_done, lin(n, 2, part + 1)))
            nc.gpsimd.tensor_scalar(ssf[:, c0:c1], ss[:, c0:c1], 1.0 / DH, RMS_FLOOR,
                                    ALU.mult, ALU.max).then_inc(floor_done, 1)
            wait(p, floor_done, lin(n, 2, part + 1))
            nc.gpsimd.tensor_tensor(rms[:, c0:c1], ssf[:, c0:c1], neghalf[:, 0:c1 - c0],
                                    ALU.pow).then_inc(rms_done, 1)
            if part == 0:
                held(p, (rms_done, lin(n, 2, 1)),
                        (masked_max, lin(n, UNITS, -UNITS)))
                nc.gpsimd.tensor_scalar(nrq[:, q, :], rms[:, KT * H:(KT + QT) * H], -float(DH) ** -0.5, None, ALU.mult).then_inc(nrq_done, 1)

        def pool_body(p, b, first=False, last=False, ahead=True):
            n, m, f = after(b, 1), after(b, -1), after(b, 2)
            if ahead:
                pool_rstd1(p, f)
            if not first:
                pool_rstd3(p, m)
            if not last:
                pool_rms(p, n, 0)
                pool_rms(p, n, 1)
            if ahead:
                pool_rstd2(p, f)
            if ahead:
                pool_xb(p, f)
            if not first:
                pool_router(p, m)
                pool_scatter(p, m)

        @block.gpsimd
        def _(p):
            nc.gpsimd.memset(neghalf[:], -0.5).then_inc(zeroed, 1)
            p.wait_ge(zeroed, 1)
            nc.gpsimd.memset(half_[:], 0.5)
            nc.gpsimd.memset(ones_f[:], 1.0)
            nc.gpsimd.memset(ones[:], 1.0)
            nc.gpsimd.memset(before[:], 0.0)
            nc.gpsimd.memset(before_b[:], 0.0)
            nc.gpsimd.memset(pad_row[:, 0:D + 1], 0.0)
            nc.gpsimd.memset(pad_row[:].bitcast(I32)[:, D + 1:ROW], NOWHERE)
            nc.gpsimd.memset(mask_u8[:, B * M:], 0)
            for q in range(2):
                ins = nc.gpsimd.memset(mbias[q][:, M:NK], 0.0)
            ins.then_inc(zeroed, 1)
            pool_rstd1(p, 0)
            pool_rstd2(p, 0)
            p.wait_ge(zeroed, 2)
            p.wait_ge(ld_const, LOADED)
            pool_xb(p, 0)
            pool_rms(p, 0, 0)
            pool_rms(p, 0, 1)
            pool_rstd1(p, 1)
            pool_rstd2(p, 1)
            pool_xb(p, 1)
            region_v = sorted_rows[0:E * REGION, :].rearrange("(e r) c -> r e c", r=REGION)
            spare_v = sorted_rows[E * REGION:, :].rearrange("(j p) c -> p j c", p=P)
            for j in range(E // 2):
                for rows in (region_v[0:P, 2 * j:2 * j + 2, :], spare_v[:, 2 * j:2 * j + 2, :]):
                    p.dma_start(rows, pad_row[:].unsqueeze(1).to_broadcast([P, 2, ROW])).then_inc(scattered[j % 2], 16)
            p.wait_ge(bias_ld, 16)
            nc.gpsimd.tensor_copy(bias_part[0][:], bias_in[:]).then_inc(bias_chain, 1)
            p.wait_ge(bias_chain, 1)
            nc.gpsimd.tensor_tensor(bias_rest[:], bias_in[:], bias_part[0][:], ALU.subtract).then_inc(bias_chain, 1)
            p.wait_ge(bias_chain, 2)
            nc.gpsimd.tensor_copy(bias_part[1][:], bias_rest[:]).then_inc(bias_chain, 1)
            p.wait_ge(bias_chain, 3)
            nc.gpsimd.tensor_tensor(bias_in[:], bias_rest[:], bias_part[1][:], ALU.subtract).then_inc(bias_chain, 1)
            p.wait_ge(bias_chain, 4)
            nc.gpsimd.tensor_copy(bias_part[2][:], bias_in[:]).then_inc(bias_chain, 1)
            pool_body(p, 0, first=True)
            with p.Fori(0, 3) as i:
                pool_body(p, (i, 1, 2))
                pool_body(p, (i, 2, 2))
            pool_body(p, 7, last=True, ahead=False)
            pool_rstd3(p, 7)
            pool_router(p, 7)
            pool_scatter(p, 7)

            def send(t):
                q = mod(t, RING)
                held(p, (y_set, lin(t, 1, 1)))
                nc.gpsimd.indirect_dma_start(
                    out=results[:, :],
                    out_offset=bass.IndirectOffsetOnAxis(ap=xt[q].bitcast(U32)[:, D + 1:ROW], axis=0),
                    in_=y[q], in_offset=None, bounds_check=B * S * TOP - 1, oob_is_err=False).then_inc(y_out[q], 16)

            tiles(p, send)
            add_results(p, nc.gpsimd, 2)

        def dve_stats(v, n):
            wait(v, rows_in[par(n)], part_of(n, 2, 32, 32))
            wait(v, norm1_done, lin(n, 2, 0))
            for t in range(QT):
                nc.vector.bn_stats(stat[:, CT + t, :], xs[par(n)][:, t, :])
            for t in range(CT):
                ins = nc.vector.bn_stats(stat[:, t, :], cs[par(n)][:, t, :])
            ins.then_inc(stat1_done, 1)
            held(v, (stat1_done, lin(n, 2, 1)))
            for t in range(CT + QT):
                ins = nc.vector.bn_aggr(mv[:, t, :], stat[:, t, :])
            ins.then_inc(stat1_done, 1)

        def dve_stats2(v, n):
            wait(v, norm1_done, lin(n, 2, 1))
            wait(v, xz_done, lin(n, 1, 0))
            for t in range(QT):
                ins = nc.vector.bn_stats(stat2[:, t, :], xhat[:, t, :])
            ins.then_inc(stat2_done, 1)
            held(v, (stat2_done, lin(n, 2, 1)))
            for t in range(QT):
                ins = nc.vector.bn_aggr(mv2[:, t, :], stat2[:, t, :])
            ins.then_inc(stat2_done, 1)

        def dve_xhat(v, n):
            q = par(n)
            wait(v, rstd1_done, lin(n, 2, 2))
            wait(v, xz_done, lin(n, 1, 0))
            for t in range(QT):
                ins = nc.vector.tensor_scalar(xhat[:, t, :], xs[q][:, t, :], mv[:, CT + t, 0:1],
                                              rstd[:, CT + t:CT + t + 1], ALU.subtract, ALU.mult)
            ins.then_inc(norm1_done, 1)

        def dve_cn(v, n):
            q = par(n)
            wait(v, prep_pe, lin(n, 8, 2 - 16))
            for t in range(CT):
                ins = nc.vector.tensor_scalar(cn[:, q, t, :], cs[q][:, t, :], mv[:, t, 0:1],
                                              rstd[:, t:t + 1], ALU.subtract, ALU.mult)
            ins.then_inc(norm1_done, 1)

        def dve_xz(v, n):
            q = par(n)
            wait(v, rstd2_done, lin(n, 2, 2))
            wait(v, prep_pe, lin(n, 8, 1 - 16))
            for t in range(QT):
                ins = nc.vector.tensor_scalar(xz[:, q, t, :], xhat[:, t, :], mv2[:, t, 0:1],
                                              rstd2[:, t:t + 1], ALU.subtract, ALU.mult)
            ins.then_inc(xz_done, 1)

        def dve_prep(v, n, step):
            q = par(n)
            wait(v, prep_pe, lin(n, 8, step + 1))
            if step == 1:
                wait(v, prep_pe, lin(n, 8, 6 - 8))
                ins = nc.vector.tensor_scalar(cT[:], M1[0:C, :], col["ln_x_g"][0:C], col["ln_x_b"][0:C], ALU.mult, ALU.add)
            if step == 3:
                wait(v, pv_done, lin(n, UNITS, -UNITS))
                ins = nc.vector.tensor_copy(kvq[q][:, CT + 1, :], M1[:, 0:3 * D])
            if step == 5:
                ins = nc.vector.tensor_copy(kvq[q][:, 2:4, 0:2 * D], M1[:].rearrange("p (t n) -> p t n", t=2))
            if step == 7:
                wait(v, scores_ready, lin(n, UNITS, -UNITS))
                ins = nc.vector.tensor_copy(kT[q][:, 0:M], M1[:])
            ins.then_inc(m1_out, 1)

        def dve_ss(v, n, part):
            wait(v, sq_done, lin(n, 2, part + 1))
            wait(v, rms_done, lin(n, 2, part + 1 - 2))
            t0, t1 = ((CT, KT + QT), (0, CT))[part]
            nc.vector.tensor_reduce(ss[:, t0 * H:t1 * H], sq[:, t0:t1, :].rearrange("p t (h d) -> p (t h) d", h=H),
                                    AX.X, ALU.add).then_inc(ss_done, 1)

        def dve_keys(v, n, part):
            wait(v, rms_done, lin(n, 2, part + 1))
            wait(v, prep_pe, lin(n, 8, part - 1))
            t0, t1 = ((CT, KT), (0, CT))[part]
            nc.vector.tensor_tensor(
                kn[:, t0:t1, :].rearrange("p t (h d) -> p t h d", h=H),
                kvq[par(n)][:, t0:t1, 0:D].rearrange("p t (h d) -> p t h d", h=H),
                rms[:, t0 * H:t1 * H].rearrange("p (t h) -> p t h", h=H).unsqueeze(3).to_broadcast([P, t1 - t0, H, DH]),
                ALU.mult).then_inc((knl_done, knc_done)[part], 1)

        def dve_max(v, b, u):
            q = u % 2
            if u == 0:
                wait(v, nrq_done, lin(b, 1, 1))
                wait(v, masked, lin(b, 1, 1))
                v.wait_ge(zeroed, 2)
            held(v, (scores_ready, lin(b, UNITS, u + 1)),
                    (prob_ready, lin(b, UNITS, u + 1 - 2)))
            nc.vector.tensor_tensor_reduce(out=sm[q][:], in0=S_ps[:, 0:NK],
                                           in1=mbias[par(b)][:],
                                           scale=nrq[:, par(b), u:u + 1], scalar=3e38, op0=ALU.add, op1=ALU.min,
                                           accum_out=negmax[:, q:q + 1]).then_inc(masked_max, 1)

        def dve_o(v, b, u):
            q, (t, h) = u % 2, divmod(u, H)
            wait(v, prob_ready, lin(b, UNITS, u + 1))
            nc.vector.reciprocal(rden[:, q:q + 1], den[:, q:q + 1]).then_inc(rden_done, 1)
            wait(v, rden_done, lin(b, UNITS, u + 1))
            wait(v, pv_done, lin(b, UNITS, u + 1))
            if u == 0:
                wait(v, post_pe, lin(b, 2, 1 - 2))
            nc.vector.tensor_scalar(o_sb[:, t, h * DH:(h + 1) * DH], O_ps[:, 0:DH], rden[:, q:q + 1], None,
                                    ALU.mult).then_inc(o_ready, 1)

        def dve_x2(v, m):
            wait(v, post_pe, lin(m, 5, 2))
            wait(v, xb_done, lin(m, 1, 1))
            rows = x2[:, bass.ds(lin(m, QT, 0), QT), :]
            nc.vector.tensor_tensor(rows, X_ps[:, 0:S].rearrange("p (t d) -> p t d", t=QT),
                                    xb[:, bass.ds(lin(m, QT, 0), QT), :], ALU.add).then_inc(x2_ready, 1)
            held(v, (x2_ready, lin(m, 1, 1)))
            for t in range(QT):
                ins = nc.vector.bn_stats(stat3[:, t, :], x2[:, bass.ds(lin(m, QT, t), 1), :].rearrange("p o d -> p (o d)"))
            ins.then_inc(stat3_done, 1)
            held(v, (stat3_done, lin(m, 2, 1)))
            for t in range(QT):
                ins = nc.vector.bn_aggr(mv3[:, t, :], stat3[:, t, :])
            ins.then_inc(stat3_done, 1)

        def dve_xf(v, m):
            q = par(m)
            wait(v, rstd3_done, lin(m, 2, 2))
            wait(v, scattered[q], part_of(m, 2, 64, 64))
            for t in range(QT):
                ins = nc.vector.tensor_scalar(
                    rows_out[q][:, t, :, 0:D],
                    x2[:, bass.ds(lin(m, QT, t), 1), :].to_broadcast([P, TOP, D]),
                    mv3[:, t, 0:1], rstd3[:, t:t + 1], ALU.subtract, ALU.mult)
            ins.then_inc(xf_done, 1)

        def dve_top(v, m):
            wait(v, post_pe, lin(m, 5, 4))
            if m == 0:
                v.wait_ge(x_free, 1)
            nc.vector.scalar_tensor_tensor(out=d2raw[:], in0=X_ps[:, 0:QT * E].rearrange("p (t e) -> p t e", t=QT),
                                           scalar=-2.0, in1=cc[:].unsqueeze(1).to_broadcast([P, QT, E]),
                                           op0=ALU.mult, op1=ALU.add).then_inc(router_done, 1)
            held(v, (router_done, lin(m, 6, 1)), (xx_done, lin(m, 1, 1)))
            for t in range(QT):
                ins = nc.vector.tensor_scalar(d2[:, t, :], d2raw[:, t, :], xx[:, t:t + 1], 1e-12, ALU.add, ALU.max)
            ins.then_inc(router_done, 1)
            held(v, (router_done, lin(m, 6, 2)))
            for t in range(QT):
                ins = nc.vector.max(best[:, t, :], d2[:, t, :])
            ins.then_inc(router_done, 1)
            held(v, (router_done, lin(m, 6, 3)))
            for t in range(QT):
                ins = nc.vector.max_index(choice[:, t, :], best[:, t, :], d2[:, t, :])
            ins.then_inc(router_done, 1)
            wait(v, router_done, lin(m, 6, 4))
            nc.vector.tensor_tensor(onehot[:], tab[:, T_IOTA:T_IOTA + E].unsqueeze(1).unsqueeze(1).to_broadcast([P, QT, TOP, E]),
                                    choice[:, :, 0:TOP].unsqueeze(3).to_broadcast([P, QT, TOP, E]),
                                    ALU.is_equal).then_inc(router_done, 1)
            wait(v, router_done, lin(m, 6, 5))
            nc.vector.tensor_tensor(picks[:], onehot[:, :, 0, :], onehot[:, :, 1, :], ALU.add).then_inc(router_done, 1)

        def dve_place(v, m):
            q = par(m)
            wait(v, post_pe, lin(m, 5, 5))
            nc.vector.tensor_tensor(ranks[:], X_ps[:, 0:QT * E].rearrange("p (t e) -> p t e", t=QT),
                                    tab[:, T_BASE:T_BASE + E].unsqueeze(1).to_broadcast([P, QT, E]), ALU.add).then_inc(x_free, 1)
            wait(v, x_free, lin(m, 1, 2))
            nc.vector.tensor_tensor(ranked[:], onehot[:], ranks[:].unsqueeze(2).to_broadcast([P, QT, TOP, E]),
                                    ALU.mult).then_inc(pos_done, 1)
            wait(v, pos_done, lin(m, 3, 1))
            nc.vector.tensor_reduce(pos_f[:], ranked[:].rearrange("p t k e -> p (t k) e"), AX.X, ALU.add).then_inc(pos_done, 1)
            nc.vector.tensor_tensor(before_t[:], before[:], picks[:, 0, :], ALU.add).then_inc(before_done, 1)
            wait(v, before_done, lin(m, 3, 1))
            nc.vector.tensor_tensor(before[:], before_t[:], picks[:, 1, :], ALU.add).then_inc(before_done, 1)
            wait(v, before_done, lin(m, 3, 2))
            nc.vector.tensor_copy(before_b[:], before[:]).then_inc(before_done, 1)
            wait(v, pos_done, lin(m, 3, 2))
            wait(v, scattered[q], part_of(m, 2, 64, 64))
            nc.vector.tensor_copy(pos[q][:], pos_f[:]).then_inc(pos_done, 1)

        def dve_weight(v, m):
            q = par(m)
            wait(v, egap_done, lin(m, 1, 1))
            nc.vector.tensor_scalar(esum[:], egap[:], 1.0, None, ALU.add).then_inc(weight_done, 1)
            wait(v, weight_done, lin(m, 3, 1))
            nc.vector.reciprocal(rows_out[q][:, :, 0, D], esum[:]).then_inc(weight_done, 1)
            wait(v, weight_done, lin(m, 3, 2))
            nc.vector.tensor_tensor(rows_out[q][:, :, 1, D], egap[:], rows_out[q][:, :, 0, D], ALU.mult).then_inc(weight_done, 1)

        def dve_split(v, e):
            wait(v, w_hi, lin(e, 1, 1))
            nc.vector.tensor_tensor(w1_lo[:, bass.ds(lin(e, 1, 0), 1), :], w1_in[:].unsqueeze(1),
                                    w1_hi[:, bass.ds(lin(e, 1, 0), 1), :].bitcast(F32), ALU.subtract)
            w2_e = w2_parts[:, bass.ds(lin(e, 1, 0), 1), :, :, :]
            nc.vector.tensor_tensor(w2_e[:, :, :, 1, :], w2_in[:].rearrange("p (o c d) -> p o c d", o=1, c=HC),
                                    w2_e[:, :, :, 0, :].bitcast(F32), ALU.subtract).then_inc(w_lo, 1)

        def dve_body(v, b, first=False, last=False, ahead=True):
            n, m, f = after(b, 1), after(b, -1), after(b, 2)
            if not last:
                dve_prep(v, n, 1)
            dve_max(v, b, 1)
            if ahead:
                dve_stats(v, f)
            dve_o(v, b, 0)
            dve_split(v, b)
            if not last:
                dve_prep(v, n, 3)
            if not first:
                dve_x2(v, m)
            dve_max(v, b, 2)
            if not last:
                dve_prep(v, n, 5)
                dve_ss(v, n, 0)
            dve_o(v, b, 1)
            if not last:
                dve_ss(v, n, 1)
            if not first:
                dve_xf(v, m)
            dve_max(v, b, 3)
            if not last:
                dve_keys(v, n, 0)
            if ahead:
                dve_xhat(v, f)
                dve_stats2(v, f)
            if not last:
                dve_keys(v, n, 1)
            dve_o(v, b, 2)
            if ahead:
                dve_cn(v, f)
            if not last:
                dve_prep(v, n, 7)
            if not first:
                dve_top(v, m)
            if ahead:
                dve_xz(v, f)
            if not last:
                dve_max(v, n, 0)
            dve_o(v, b, 3)
            if not first:
                dve_place(v, m)
                dve_weight(v, m)

        @block.vector
        def _(v):
            dve_stats(v, 0)
            dve_xhat(v, 0)
            dve_stats2(v, 0)
            dve_cn(v, 0)
            dve_xz(v, 0)
            v.wait_ge(ld_const, LOADED)
            nc.vector.tensor_tensor(gqk[:], col["qn_g"], col["kn_g"], ALU.mult).then_inc(gqk_done, 1)
            nc.vector.tensor_tensor(cen2[:], cenT[:], cenT[:], ALU.mult).then_inc(setup_v, 1)
            nc.vector.tensor_copy(triu[:], triu_f[:]).then_inc(setup_v, 1)
            dve_prep(v, 0, 1)
            dve_prep(v, 0, 3)
            dve_prep(v, 0, 5)
            dve_ss(v, 0, 0)
            dve_stats(v, 1)
            dve_ss(v, 0, 1)
            dve_keys(v, 0, 0)
            dve_keys(v, 0, 1)
            dve_prep(v, 0, 7)
            dve_xhat(v, 1)
            dve_stats2(v, 1)
            dve_cn(v, 1)
            dve_max(v, 0, 0)
            dve_xz(v, 1)
            v.wait_ge(setup_t, 1)
            nc.vector.tensor_copy(cc[:], X_ps[:, 0:E]).then_inc(x_free, 1)
            dve_body(v, 0, first=True)
            with v.Fori(0, 3) as i:
                dve_body(v, (i, 1, 2))
                dve_body(v, (i, 2, 2))
            dve_body(v, 7, last=True, ahead=False)
            dve_x2(v, 7)
            dve_xf(v, 7)
            dve_top(v, 7)
            dve_place(v, 7)
            dve_weight(v, 7)

            step = [0]

            def chain(ins):
                step[0] += 1
                ins.then_inc(table, 1)
                v.wait_ge(table, step[0])

            v.wait_ge(counted, 1)
            chain(nc.vector.tensor_copy(counts[:], X_ps[:, 0:E]))
            chain(nc.vector.tensor_tensor(fills[:], counts[:].unsqueeze(2).to_broadcast([P, E, B * S // P]),
                                          tab[:, T_FILL:T_POW].unsqueeze(1).to_broadcast([P, E, B * S // P]), ALU.is_gt))
            chain(nc.vector.tensor_reduce(ntiles[:], fills[:], AX.X, ALU.add))
            nc.vector.tensor_copy(ends[:, E:], tab[:, T_BASE + E:T_TRI])
            nc.vector.tensor_tensor(ends[:, 0:E], counts[:], tab[:, T_BASE:T_BASE + E], ALU.add)
            chain(nc.vector.tensor_tensor(cum_terms[:], ntiles[:].unsqueeze(1).to_broadcast([P, E + 1, E]),
                                          tab[:, T_TRI:T_TILE].rearrange("p (e f) -> p e f", f=E), ALU.mult))
            chain(nc.vector.tensor_reduce(cum[:], cum_terms[:], AX.X, ALU.add))
            nc.vector.scalar_tensor_tensor(out=offset[:], in0=cum[:], scalar=-float(P), in1=ends[:], op0=ALU.mult, op1=ALU.add)
            chain(nc.vector.tensor_tensor(passed, tab[:, T_TILE:T_ROWS].unsqueeze(2).to_broadcast([P, TILES, E]),
                                          cum[:, 0:E].unsqueeze(1).to_broadcast([P, TILES, E]), ALU.is_ge))
            nc.vector.tensor_tensor(jump[:], offset[:, 1:], offset[:, 0:E], ALU.subtract)
            chain(nc.vector.tensor_reduce(expert[:], passed, AX.X, ALU.add))
            nc.vector.tensor_scalar(expert_at[:], expert[:], float(E - 1), None, ALU.min)
            chain(nc.vector.tensor_scalar(expert[:], expert[:], float(E - 1), None, ALU.min))
            in_groups = expert[:, TILES - 1 - GROUPS * RING:TILES - 1].rearrange("p (g k) -> p g k", k=RING)
            chain(nc.vector.tensor_tensor(digits[:], in_groups, tab[:, T_POW:TAB].unsqueeze(1).to_broadcast([P, GROUPS, RING]), ALU.mult))
            chain(nc.vector.tensor_reduce(grouped[:], digits[:], AX.X, ALU.add))
            chain(nc.vector.tensor_tensor(start_terms, passed, jump[:].unsqueeze(1).to_broadcast([P, TILES, E]), ALU.mult))
            nc.vector.tensor_copy(group_at[:], grouped[:])
            chain(nc.vector.tensor_reduce(start[:], start_terms, AX.X, ALU.add))
            nc.vector.scalar_tensor_tensor(out=row_at[:], in0=start[:], scalar=offset[:, 0:1], in1=tab[:, T_ROWS:T_FILL],
                                           op0=ALU.add, op1=ALU.add).then_inc(table, 1)
            assert step[0] + 1 == TABLE_STEPS

            def xT_step(t):
                q = mod(t, 2)
                wait(v, xT_pe, lin(t, 1, 1))
                wait(v, gu_pe, lin(t, 1, 1 - 2))
                nc.vector.tensor_copy(xT_hi[q][:], XT_ps).then_inc(xT_hi_set, 1)
                wait(v, xT_hi_set, lin(t, 1, 1))
                nc.vector.tensor_tensor(xT_lo[q][:], XT_ps, xT_hi[q][:].bitcast(F32), ALU.subtract).then_inc(xT_lo_set, 1)

            def hid_step(t):
                q = mod(t, 2)
                wait(v, gate_set, lin(t, 1, 1))
                wait(v, hT_pe, lin(t, 1, 1 - 2))
                nc.vector.tensor_tensor(hid[q], U_ps[q], gate[q], ALU.mult).then_inc(hid_set, 1)

            def hT_step(t):
                q = mod(t, 2)
                wait(v, hT_hi_set, lin(t, 1, 1))
                nc.vector.tensor_tensor(hT_lo[q][:], HT_ps[q][0:HP, 0:HC * P], hT_hi[q][:].bitcast(F32), ALU.subtract).then_inc(hT_lo_set, 1)

            def y_step(t):
                r_ = mod(t, RING)
                wait(v, y_half, lin(t, 1, 1))
                nc.vector.scalar_tensor_tensor(out=y[r_], in0=Y_ps[:, D:2 * D], scalar=xt[r_][:, D:D + 1],
                                               in1=y[r_], op0=ALU.mult, op1=ALU.add).then_inc(y_set, 1)

            def tile(t):
                if t != TILES - 1:
                    xT_step(after(t, 1))
                if t not in (0, 1, 2):
                    y_step(after(t, -3))
                hid_step(t)
                if t != 0:
                    hT_step(after(t, -1))

            xT_step(0)
            tiles(v, tile)
            hT_step(TILES - 1)
            for t in range(TILES - 3, TILES):
                y_step(t)
            for j in (0, 1, 3):
                add_results(v, nc.vector, j)

        def act_prep(s, n, step):
            q = par(n)
            wait(s, prep_pe, lin(n, 8, step + 1))
            if step == 0:
                wait(s, prep_pe, lin(n, 8, 4 - 8))
                ins = nc.scalar.activation(lnT[:], M0[:, 0:S], ACT.Identity, bias=col["ln_l_b"], scale=col["ln_l_g"])
            if step == 2:
                wait(s, pv_done, lin(n, UNITS, -UNITS))
                ins = nc.scalar.copy(kvq[q][:, CT, :], M0[:, 0:3 * D])
            if step == 4:
                ins = nc.scalar.copy(kvq[q][:, 0:2, 0:2 * D], M0[:].rearrange("p (t n) -> p t n", t=2))
            if step == 6:
                wait(s, scores_ready, lin(n, UNITS, -UNITS))
                nc.scalar.activation(qT[q][:], M0[:, 0:S], ACT.Copy, scale=gqk[:])
                ins = nc.scalar.copy(kT[q][:, M:NK], M0[:, S:2 * S])
            ins.then_inc(m0_out, 1)

        def act_sq(s, n, part):
            q = par(n)
            wait(s, m0_out, lin(n, 4, part + 2))
            wait(s, m1_out, lin(n, 4, part + 2))
            wait(s, ss_done, lin(n, 2, part - 1))
            if part == 0:
                nc.scalar.activation(sq[:, KT:KT + QT, :], kvq[q][:, CT:KT, 2 * D:3 * D], ACT.Square)
            t0, t1 = ((CT, KT), (0, CT))[part]
            nc.scalar.activation(sq[:, t0:t1, :], kvq[q][:, t0:t1, 0:D], ACT.Square).then_inc(sq_done, 1)

        def act_exp(s, b, u):
            q = u % 2
            wait(s, masked_max, lin(b, UNITS, u + 1))
            wait(s, tb_ready, lin(b, UNITS, u + 1 - 2))
            wait(s, rden_done, lin(b, UNITS, u + 1 - 2))
            nc.scalar.activation(prob[q][:], sm[q][:], ACT.Exp, bias=negmax[:, q:q + 1], scale=-1.0,
                                 accum_out=den[:, q:q + 1]).then_inc(prob_ready, 1)

        def act_pT(s, b, u):
            q = u % 2
            wait(s, ta_ready, lin(b, UNITS, u + 1))
            wait(s, pv_done, lin(b, UNITS, u + 1 - 2))
            nc.scalar.copy(pT[q][:, 0:3 * P], Ta[:, 0:3 * P]).then_inc(pa_ready, 1)
            wait(s, tb_ready, lin(b, UNITS, u + 1))
            nc.scalar.copy(pT[q][:, 3 * P:], Tb[:, 0:3 * P]).then_inc(pb_ready, 1)

        def act_mask(s, b):
            wait(s, masked_max, lin(b, UNITS, -UNITS))
            s.wait_ge(ld_const, LOADED)
            nc.scalar.activation(mbias[par(b)][:, 0:M], mask_u8[:, bass.ds(lin(b, M, 0), M)], ACT.Copy,
                                 bias=-BIG, scale=BIG).then_inc(masked, 1)

        def act_oT(s, m):
            wait(s, post_pe, lin(m, 5, 1))
            nc.scalar.copy(oT[:], X_ps[:, 0:S]).then_inc(oT_ready, 1)

        def act_xf(s, m):
            wait(s, post_pe, lin(m, 5, 3))
            nc.scalar.copy(xfT[:], X_ps[:, 0:S]).then_inc(xfT_ready, 1)
            for t in range(QT):
                ins = nc.scalar.activation(square_scrap[:, t, :], rows_out[par(m)][:, t, 0, 0:D], ACT.Square, accum_out=xx[:, t:t + 1])
            ins.then_inc(xx_done, 1)

        def act_gap(s, m):
            wait(s, dist_done, lin(m, 2, 2))
            nc.scalar.activation(egap[:], dgap[:], ACT.Exp).then_inc(egap_done, 1)

        def act_split(s, e):
            wait(s, w_in, lin(e, 32, 32))
            nc.scalar.copy(w1_hi[:, bass.ds(lin(e, 1, 0), 1), :], w1_in[:].unsqueeze(1))
            nc.scalar.copy(w2_parts[:, bass.ds(lin(e, 1, 0), 1), :, 0, :],
                           w2_in[:].rearrange("p (o c d) -> p o c d", o=1, c=HC)).then_inc(w_hi, 1)

        def act_body(s, b, first=False, last=False, ahead=True):
            n, m = after(b, 1), after(b, -1)
            if not last:
                act_prep(s, n, 0)
            act_pT(s, b, 0)
            act_split(s, b)
            act_exp(s, b, 1)
            if not first:
                act_oT(s, m)
            if not last:
                act_prep(s, n, 2)
            act_pT(s, b, 1)
            if not last:
                act_prep(s, n, 4)
                act_sq(s, n, 0)
            act_exp(s, b, 2)
            if not last:
                act_sq(s, n, 1)
            act_pT(s, b, 2)
            if not first:
                act_xf(s, m)
            act_exp(s, b, 3)
            if not last:
                act_prep(s, n, 6)
            act_pT(s, b, 3)
            if not last:
                act_exp(s, n, 0)
            if ahead:
                act_mask(s, after(b, 2))
            if not first:
                act_gap(s, m)

        @block.scalar
        def _(s):
            s.wait_ge(ld_const, LOADED)
            s.wait_ge(zeroed, 2)
            act_mask(s, 0)
            act_mask(s, 1)
            act_prep(s, 0, 0)
            act_prep(s, 0, 2)
            act_sq(s, 0, 0)
            act_prep(s, 0, 4)
            act_sq(s, 0, 1)
            s.wait_ge(gqk_done, 1)
            act_prep(s, 0, 6)
            act_exp(s, 0, 0)
            act_body(s, 0, first=True)
            with s.Fori(0, 3) as i:
                act_body(s, (i, 1, 2))
                act_body(s, (i, 2, 2))
            act_body(s, 7, last=True, ahead=False)
            act_oT(s, 7)
            act_xf(s, 7)
            act_gap(s, 7)

            def gate_step(t):
                q = mod(t, 2)
                wait(s, gu_pe, lin(t, 1, 1))
                wait(s, hid_set, lin(t, 1, 1 - 2))
                nc.scalar.activation(gate[q], G_ps[q], ACT.Silu).then_inc(gate_set, 1)

            def hT_step(t):
                q = mod(t, 2)
                wait(s, hT_pe, lin(t, 1, 1))
                wait(s, y_pe, lin(t, 1, 1 - 2))
                nc.scalar.copy(hT_hi[q][:], HT_ps[q][0:HP, 0:HC * P]).then_inc(hT_hi_set, 1)

            def y_step(t):
                q = mod(t, RING)
                wait(s, y_pe, lin(t, 1, 1))
                wait(s, y_out[q], part_of(t, RING, 16, 0))
                nc.scalar.activation(y[q], Y_ps[:, 0:D], ACT.Copy, scale=xt[q][:, D:D + 1]).then_inc(y_half, 1)

            def tile(t):
                gate_step(t)
                if t != 0:
                    hT_step(after(t, -1))
                if t not in (0, 1):
                    y_step(after(t, -2))

            tiles(s, tile)
            hT_step(TILES - 1)
            y_step(TILES - 2)
            y_step(TILES - 1)

        def pe_prep(t_, n, step):
            q = par(n)
            bank_ = (M0, M1)[step % 2]
            wait(t_, (m0_out, m1_out)[step % 2], lin(n, 4, step // 2))
            if step == 0:
                wait(t_, xz_done, lin(n, 1, 1))
                for t in range(QT):
                    ins = nc.tensor.transpose(bank_[:, t * P:(t + 1) * P], xz[:, q, t, :], eye[:])
            if step == 1:
                wait(t_, norm1_done, lin(n, 2, 2))
                for t in range(CT):
                    ins = nc.tensor.transpose(bank_[0:C, t * P:(t + 1) * P], cn[:, q, t, :], eye[:])
            if step in (2, 3):
                if step == 2:
                    wait(t_, m0_out, lin(n, 4, 1))
                t = step - 2
                ins = nc.tensor.matmul(bank_[:, 0:3 * D], lnT[:, t * P:(t + 1) * P], wqkv_l[:], start=True, stop=True)
            if step in (4, 5):
                if step == 4:
                    wait(t_, m1_out, lin(n, 4, 1))
                for j in range(2):
                    t = 2 * (step - 4) + j
                    ins = nc.tensor.matmul(bank_[:, j * 2 * D:(j + 1) * 2 * D], cT[:, t * P:(t + 1) * P], wkv_c[:],
                                           start=True, stop=True)
            if step == 6:
                wait(t_, knl_done, lin(n, 1, 1))
                for t in range(QT):
                    nc.tensor.transpose(bank_[:, t * P:(t + 1) * P], kvq[q][:, CT + t, 2 * D:3 * D], eye[:])
                for t in range(QT):
                    ins = nc.tensor.transpose(bank_[:, S + t * P:S + (t + 1) * P], kn[:, CT + t, :], eye[:])
            if step == 7:
                wait(t_, knc_done, lin(n, 1, 1))
                for t in range(CT):
                    ins = nc.tensor.transpose(bank_[:, t * P:(t + 1) * P], kn[:, t, :], eye[:])
            ins.then_inc(prep_pe, 1)

        def pe_scores(t_, b, u):
            q, (t, h) = par(b), divmod(u, H)
            if u == 0:
                wait(t_, m0_out, lin(b, 4, 4))
                wait(t_, m1_out, lin(b, 4, 4))
            wait(t_, masked_max, lin(b, UNITS, u))
            r = slice(h * DH, (h + 1) * DH)
            nc.tensor.matmul(S_ps[:, 0:M], qT[q][r, t * P:(t + 1) * P], kT[q][r, 0:M], start=True, stop=True)
            nc.tensor.matmul(S_ps[:, M:NK], qT[q][r, t * P:(t + 1) * P], kT[q][r, M:NK], start=True,
                             stop=True).then_inc(scores_ready, 1)

        def pe_pT(t_, b, u):
            q = u % 2
            wait(t_, prob_ready, lin(b, UNITS, u + 1))
            wait(t_, pa_ready, lin(b, UNITS, u))
            for j in range(3):
                ins = nc.tensor.transpose(Ta[:, j * P:(j + 1) * P], prob[q][:, j * P:(j + 1) * P], eye[:])
            ins.then_inc(ta_ready, 1)
            wait(t_, pb_ready, lin(b, UNITS, u))
            for j in range(3):
                ins = nc.tensor.transpose(Tb[:, j * P:(j + 1) * P], prob[q][:, (3 + j) * P:(4 + j) * P], eye[:])
            ins.then_inc(tb_ready, 1)

        def pe_pv(t_, b, u):
            q, (t, h) = u % 2, divmod(u, H)
            wait(t_, pa_ready, lin(b, UNITS, u + 1))
            wait(t_, pb_ready, lin(b, UNITS, u + 1))
            wait(t_, o_ready, lin(b, UNITS, u))
            for j in range(KT):
                ins = nc.tensor.matmul(O_ps[:, 0:DH], pT[q][:, j * P:(j + 1) * P],
                                       kvq[par(b)][:, j, D + h * DH:D + (h + 1) * DH], start=(j == 0), stop=(j == KT - 1))
            ins.then_inc(pv_done, 1)

        def pe_post(t_, m, step):
            if step == 0:
                wait(t_, o_ready, lin(m, UNITS, UNITS))
                wait(t_, x_free, lin(m, 1, 1))
                for t in range(QT):
                    ins = nc.tensor.transpose(X_ps[:, t * P:(t + 1) * P], o_sb[:, t, :], eye[:])
            if step == 1:
                wait(t_, oT_ready, lin(m, 1, 1))
                for t in range(QT):
                    ins = nc.tensor.matmul(X_ps[:, t * D:(t + 1) * D], oT[:, t * P:(t + 1) * P], wo[:], start=True, stop=True)
            if step == 2:
                wait(t_, xf_done, lin(m, 1, 1))
                for t in range(QT):
                    ins = nc.tensor.transpose(X_ps[:, t * P:(t + 1) * P], rows_out[par(m)][:, t, 0, 0:D], eye[:])
            if step == 3:
                wait(t_, xfT_ready, lin(m, 1, 1))
                for t in range(QT):
                    ins = nc.tensor.matmul(X_ps[:, t * E:(t + 1) * E], xfT[:, t * P:(t + 1) * P], cenT[:], start=True, stop=True)
            if step == 4:
                wait(t_, router_done, lin(m, 6, 6))
                nc.tensor.matmul(X_ps[:, 0:E], triu[:], picks[:, 0, :], start=True, stop=False)
                nc.tensor.matmul(X_ps[:, 0:E], ones[:], before_b[:], start=False, stop=True)
                nc.tensor.matmul(X_ps[:, E:2 * E], triu[:], picks[:, 1, :], start=True, stop=False)
                nc.tensor.matmul(X_ps[:, E:2 * E], ones[:], picks[:, 0, :], start=False, stop=False)
                ins = nc.tensor.matmul(X_ps[:, E:2 * E], ones[:], before_b[:], start=False, stop=True)
            ins.then_inc(post_pe, 1)

        def pe_body(t_, b, first=False, last=False):
            n, m = after(b, 1), after(b, -1)
            if not last:
                pe_prep(t_, n, 0)
                pe_prep(t_, n, 1)
            if not first:
                pe_post(t_, m, 0)
            pe_pT(t_, b, 0)
            pe_scores(t_, b, 1)
            pe_pv(t_, b, 0)
            if not last:
                pe_prep(t_, n, 2)
                pe_prep(t_, n, 3)
            pe_pT(t_, b, 1)
            if not first:
                pe_post(t_, m, 1)
            if not last:
                pe_prep(t_, n, 4)
            pe_scores(t_, b, 2)
            if not last:
                pe_prep(t_, n, 5)
            pe_pv(t_, b, 1)
            pe_pT(t_, b, 2)
            pe_scores(t_, b, 3)
            if not first:
                pe_post(t_, m, 2)
            pe_pv(t_, b, 2)
            if not last:
                pe_prep(t_, n, 6)
            pe_pT(t_, b, 3)
            if not first:
                pe_post(t_, m, 3)
            if not last:
                pe_prep(t_, n, 7)
            pe_pv(t_, b, 3)
            if not last:
                pe_scores(t_, n, 0)
            if not first:
                pe_post(t_, m, 4)

        @block.tensor
        def _(t_):
            t_.wait_ge(ld_const, LOADED)
            for step in range(8):
                pe_prep(t_, 0, step)
            pe_scores(t_, 0, 0)
            t_.wait_ge(setup_v, 2)
            nc.tensor.matmul(X_ps[:, 0:E], ones_f[:], cen2[:], start=True, stop=True).then_inc(setup_t, 1)
            pe_body(t_, 0, first=True)
            with t_.Fori(0, 3) as i:
                pe_body(t_, (i, 1, 2))
                pe_body(t_, (i, 2, 2))
            pe_body(t_, 7, last=True)
            for step in range(5):
                pe_post(t_, 7, step)
            t_.wait_ge(before_done, 3 * B)
            nc.tensor.matmul(X_ps[:, 0:E], ones[:], before_b[:], start=True, stop=True).then_inc(counted, 1)

            def expert_of(t):
                return t_.value_load(expert_at[0:1, bass.ds(lin(t, 1, 0), 1)], min_val=0, max_val=E - 1)

            def xT_step(t):
                wait(t_, xt_in[mod(t, RING)], part_of(t, RING, 16, 16))
                wait(t_, xT_lo_set, lin(t, 1, 0))
                nc.tensor.transpose(XT_ps, xt[mod(t, RING)][:, 0:D], eye[:]).then_inc(xT_pe, 1)

            def gu_step(t, e):
                q = mod(t, 2)
                wait(t_, xT_lo_set, lin(t, 1, 1))
                wait(t_, hid_set, lin(t, 1, 1 - 2))
                for o, at in ((G_ps[q], 0), (U_ps[q], HID)):
                    nc.tensor.matmul(o, ones[0:3, :], bias[:, bass.ds(e, 1), at:at + HID].rearrange("p o n -> p (o n)"),
                                     start=True, stop=False)
                    for n, (x_, w_) in enumerate(((xT_hi, w1_hi), (xT_hi, w1_lo), (xT_lo, w1_hi))):
                        ins = nc.tensor.matmul(o, x_[q][:], w_[:, bass.ds(e, 1), at:at + HID].rearrange("p o n -> p (o n)"),
                                               start=False, stop=(n == 2))
                ins.then_inc(gu_pe, 1)

            def hT_step(t):
                q = mod(t, 2)
                wait(t_, hid_set, lin(t, 1, 1))
                wait(t_, hT_lo_set, lin(t, 1, -1))
                for c in range(HC):
                    ins = nc.tensor.transpose(HT_ps[q][0:HP, c * P:(c + 1) * P], hid[q][:, c * HP:(c + 1) * HP], eye[:])
                ins.then_inc(hT_pe, 1)

            def y_step(t, e):
                q = mod(t, 2)
                wait(t_, hT_lo_set, lin(t, 1, 1))
                wait(t_, y_set, lin(t, 1, 0))
                for c in range(HC):
                    piece = w2_parts[:, bass.ds(e, 1), c, :, :].rearrange("p o k d -> p (o k d)")
                    nc.tensor.matmul(Y_ps, hT_hi[q][:, c * P:(c + 1) * P], piece, start=(c == 0), stop=False)
                    nc.tensor.matmul(Y_ps[:, 0:D], hT_lo[q][:, c * P:(c + 1) * P], piece[:, 0:D], start=False, stop=False)
                nc.tensor.matmul(Y_ps[:, 0:D], ones[0:3, :], bias[:, bass.ds(e, 1), 2 * HID:].rearrange("p o n -> p (o n)"),
                                 start=False, stop=True).then_inc(y_pe, 1)

            t_.wait_ge(table, TABLE_STEPS)
            t_.wait_ge(w_lo, E)
            t_.wait_ge(bias_set, 16 * 3)
            xT_step(0)

            def group(g):
                n = t_.value_load(group_at[0:1, bass.ds(lin(g, 1, 0), 1)], min_val=0, max_val=E ** RING - 1)
                return [(n >> (3 * k)) & (E - 1) for k in range(RING)]

            experts = {}

            def tile(t):
                if isinstance(t, int):
                    if t < FIRST - RING:
                        experts[t] = expert_of(t)
                    elif t == FIRST - RING:
                        experts.update(zip(range(t, FIRST), group(0)))
                    elif t == TILES - 1:
                        experts.update(zip(range(t - RING, t), group(GROUPS - 1)))
                        experts[t] = expert_of(t)
                elif t[1] == FIRST:
                    experts.update(zip(range(FIRST - RING, FIRST), group((t[0], 0, 1))))
                    experts.update(zip(range(FIRST, FIRST + RING), group((t[0], 1, 1))))
                at = t if isinstance(t, int) else t[1]
                if t != TILES - 1:
                    xT_step(after(t, 1))
                gu_step(t, experts[at])
                if t != 0:
                    hT_step(after(t, -1))
                if t not in (0, 1):
                    y_step(after(t, -2), experts[at - 2])

            tiles(t_, tile)
            hT_step(TILES - 1)
            y_step(TILES - 2, experts[TILES - 2])
            y_step(TILES - 1, experts[TILES - 1])


def kernel(**inputs):
    import concourse.bacc as bacc
    from concourse.bass_utils import run_bass_kernel_spmd

    g = {k: np.asarray(v) for k, v in inputs.items()}
    xa = {k[len("L0_xattn_"):]: v for k, v in g.items() if k.startswith("L0_xattn_")}
    fa = {k[len("L0_ffn_"):]: v for k, v in g.items() if k.startswith("L0_ffn_")}
    two = lambda v: np.concatenate([v, v])
    wide = lambda v: np.concatenate([v, np.zeros(P - v.shape[0], v.dtype)])
    arrays = {
        "x": g["x"].reshape(B * S, D),
        "ctx": g["ctx_768"].reshape(B * M, C),
        "mask": g["mask_BxS2_bk0"],
        "wqkv_l": np.concatenate([xa["Wlkv"], xa["Wq"]]).T,
        "wkv_c": xa["Wkv"].T,
        "wo": xa["Wo"].T,
        "bo": xa["bo"],
        "cols": np.stack([wide(xa["ln_x_g"]), wide(xa["ln_x_b"]), xa["ln_l_g"], xa["ln_l_b"],
                          two(xa["qn_g"]), two(xa["kn_g"])], axis=1),
        "tab": np.broadcast_to(np.concatenate([
            np.arange(E), REGION * np.arange(E) + P, [E * REGION], np.tri(E + 1, E).reshape(-1),
            np.arange(TILES), P * np.arange(TILES), P * np.arange(B * S // P), float(E) ** np.arange(RING)]).astype(np.float32), (P, TAB)),
        "slot_tab": (TOP * (P * np.arange(B * QT)[None, :, None] + np.arange(P)[:, None, None])
                     + np.arange(TOP)[None, None, :]).astype(np.int32),
        "triu": np.triu(np.ones((P, P), np.float32), 1),
        "cenT": fa["centroid"].T,
        "w1": np.concatenate([fa["Wg"], fa["W1"]], axis=2).transpose(1, 0, 2).reshape(D, E * 2 * HID),
        "w2": fa["W2"].reshape(E, HC, HP, D).transpose(2, 0, 1, 3).reshape(HP, E * HC * D),
        "bias": np.concatenate([fa["bg"], fa["b1"], fa["b2"]], axis=1).reshape(-1),
        "eye": np.eye(P, dtype=np.float32),
    }
    arrays = {k: np.ascontiguousarray(v) for k, v in arrays.items()}
    nc = bacc.Bacc("TRN2", target_bir_lowering=False, num_devices=1)
    dram = {k: nc.dram_tensor(f"in_{k}", v.shape, mybir.dt.from_np(v.dtype), kind="ExternalInput").ap()
            for k, v in arrays.items()}
    out = nc.dram_tensor("out_0", (B * S, D), F32, kind="ExternalOutput").ap()
    build(nc, dram, out)
    r = run_bass_kernel_spmd(nc, [{f"in_{k}": v for k, v in arrays.items()}], core_ids=[0])
    return r.results[0]["out_0"].reshape(B, S, D)
```
